# Optimizing a Trainium2 kernel written in Bass

```python
import numpy as np
import jax
import jax.numpy as jnp

def _softmax(x, axis=-1):
    return jax.nn.softmax(x, axis=axis)

def _gelu(x):
    return jax.nn.gelu(x, approximate=True)

def _silu(x):
    return jax.nn.silu(x)

def _sigmoid(x):
    return jax.nn.sigmoid(x)

def _layernorm(x, axis=-1, eps=1e-05):
    m = jnp.mean(x, axis=axis, keepdims=True)
    v = jnp.var(x, axis=axis, keepdims=True)
    return (x - m) / jnp.sqrt(v + eps)

def _scatter_add(tgt, idx, src, axis=0):
    return tgt.at[idx].add(src)

def _segment_sum(src, seg, n):
    return jax.ops.segment_sum(src, seg, n)
kernel_name = 'mk_decoder_postln_d1_seqx_r4_edcf94'

def setup_inputs(seed: int=0):
    np.random.seed(seed)
    _w = jnp.asarray

    def _rec_inputs():
        import jax
        import jax.numpy as jnp
        _rk = jax.random.key(seed)
        x = 7.22e-05 + 1 * jax.random.normal(jax.random.fold_in(_rk, 1), (64, 128, 512), jnp.float32)
        _lenS = 128 - jax.random.randint(jax.random.fold_in(_rk, 7), (64,), 0, max(1, 128 // 4) + 1, jnp.int32)
        _lenS2 = 128 - jax.random.randint(jax.random.fold_in(_rk, 8), (64,), 0, max(1, 128 // 4) + 1, jnp.int32)
        _ctx_2048P = jax.random.normal(jax.random.fold_in(_rk, 11), (64, 16, 512), jnp.float32)
        _ctx_2048c = jax.random.dirichlet(jax.random.fold_in(_rk, 511), 0.3 * jnp.ones((16,), jnp.float32), (64, 128))
        _ctx_2048t = jnp.einsum('bsk,bkd->bsd', _ctx_2048c, _ctx_2048P)
        _ctx_2048t = _ctx_2048t * jax.lax.rsqrt(jnp.mean(jnp.square(_ctx_2048t)) + 1e-12) * 0.953939
        ctx_2048 = 4.13588e-05 + 0.999923 * (_ctx_2048t + 0.3 * jax.random.normal(jax.random.fold_in(_rk, 611), (64, 128, 512), jnp.float32))
        return (x, ctx_2048)
    x, ctx_2048 = _rec_inputs()

    def _L0_attn_setup():
        import jax, jax.numpy as jnp
        import numpy as np
        B, S, H = (2, 512, 512)
        NH, HD = (16, H // 16)
        WINDOW = 256
        THETA = 10000.0
        EPS = 1e-06

        def rmsnorm(x, w):
            var = jnp.mean(jnp.square(x), axis=-1, keepdims=True)
            return x * jax.lax.rsqrt(var + EPS) * w

        def rope(x, cos, sin):
            d2 = x.shape[-1] // 2
            x1, x2 = (x[..., :d2], x[..., d2:])
            c = cos[None, :, None, :]
            s = sin[None, :, None, :]
            return jnp.concatenate([x1 * c - x2 * s, x2 * c + x1 * s], axis=-1)
        key = jax.random.key(seed)
        k1, k2, k3 = jax.random.split(key, 3)
        sc = 1.0 / np.sqrt(H)
        return {'hidden_states': jax.random.normal(k1, (B, S, H), dtype=jnp.float32), 'Wqkv': jax.random.normal(k2, (H, 3 * H), dtype=jnp.float32) * sc, 'q_norm_w': jnp.ones((H,), dtype=jnp.float32), 'k_norm_w': jnp.ones((H,), dtype=jnp.float32), 'Wo': jax.random.normal(k3, (H, H), dtype=jnp.float32) * sc}
    _L0_attn_all = _L0_attn_setup()
    _L0_attn_in = {k: v for k, v in _L0_attn_all.items() if k in ('Wqkv', 'q_norm_w', 'k_norm_w', 'Wo')}
    del _L0_attn_all

    def _L0_xattn_setup():
        import jax, jax.numpy as jnp
        import numpy as np
        N_HEAD = 8
        key = jax.random.key(seed)
        k1, k2, k3 = jax.random.split(key, 3)
        b, d, m = (4, 256, 512)
        c, n = (256, 512)
        q = jax.random.normal(k1, (b, d, m), dtype=jnp.float32)
        k = jax.random.normal(k2, (d // d * b, d, n), dtype=jnp.float32).reshape(b, d, n)
        v = jax.random.normal(k3, (b, c, n), dtype=jnp.float32)
        return {'q': q, 'k': k, 'v': v}
    _L0_xattn_all = _L0_xattn_setup()
    _L0_xattn_in = {k: v for k, v in _L0_xattn_all.items() if k in ()}
    del _L0_xattn_all

    def _L0_ffn_setup():
        import jax, jax.numpy as jnp
        import numpy as np
        BLOCK = 128
        MAXVAL = 448.0

        def _quant_dequant(x_flat):
            xb = x_flat.reshape(-1, BLOCK)
            s = jnp.max(jnp.abs(xb), axis=1, keepdims=True) / MAXVAL
            q = (xb / s).astype(jnp.float8_e4m3fn)
            return (q.astype(jnp.float32) * s).reshape(x_flat.shape)
        key = jax.random.key(seed)
        k1, k2 = jax.random.split(key)
        B, T, D, OUT = (4, 1024, 512, 512)
        x = jax.random.normal(k1, (B, T, D), dtype=jnp.float32)
        limit = float(np.sqrt(6.0 / (D + OUT)))
        weight = jax.random.uniform(k2, (OUT, D), minval=-limit, maxval=limit, dtype=jnp.float32)
        return {'x': x, 'weight': weight}
    _L0_ffn_all = _L0_ffn_setup()
    _L0_ffn_in = {k: v for k, v in _L0_ffn_all.items() if k in ('weight',)}
    del _L0_ffn_all
    return {'x': x, 'ctx_2048': ctx_2048, 'L0_attn_Wqkv': _L0_attn_in['Wqkv'], 'L0_attn_q_norm_w': _L0_attn_in['q_norm_w'], 'L0_attn_k_norm_w': _L0_attn_in['k_norm_w'], 'L0_attn_Wo': _L0_attn_in['Wo'], 'L0_ffn_weight': _L0_ffn_in['weight']}

def reference(x, ctx_2048, L0_attn_Wqkv, L0_attn_q_norm_w, L0_attn_k_norm_w, L0_attn_Wo, L0_ffn_weight):
    import jax
    import jax.numpy as jnp

    def _L0_attn_ref(hidden_states, Wqkv, q_norm_w, k_norm_w, Wo):
        import jax, jax.numpy as jnp
        import numpy as np
        B, S, H = (2, 512, 512)
        NH, HD = (16, H // 16)
        WINDOW = 256
        THETA = 10000.0
        EPS = 1e-06

        def rmsnorm(x, w):
            var = jnp.mean(jnp.square(x), axis=-1, keepdims=True)
            return x * jax.lax.rsqrt(var + EPS) * w

        def rope(x, cos, sin):
            d2 = x.shape[-1] // 2
            x1, x2 = (x[..., :d2], x[..., d2:])
            c = cos[None, :, None, :]
            s = sin[None, :, None, :]
            return jnp.concatenate([x1 * c - x2 * s, x2 * c + x1 * s], axis=-1)
        b, s, h = hidden_states.shape
        qkv = hidden_states @ Wqkv
        q, k, v = jnp.split(qkv, 3, axis=-1)
        q = rmsnorm(q, q_norm_w)
        k = rmsnorm(k, k_norm_w)
        q = q.reshape(b, s, NH, HD)
        k = k.reshape(b, s, NH, HD)
        v = v.reshape(b, s, NH, HD)
        inv_freq = 1.0 / THETA ** (jnp.arange(0, HD, 2, dtype=jnp.float32) / HD)
        freqs = jnp.arange(s, dtype=jnp.float32)[:, None] * inv_freq[None, :]
        cos, sin = (jnp.cos(freqs), jnp.sin(freqs))
        q = rope(q, cos, sin)
        k = rope(k, cos, sin)
        q_idx = jnp.arange(s)[:, None]
        k_idx = jnp.arange(s)[None, :]
        mask = (q_idx >= k_idx) & (q_idx - k_idx <= WINDOW - 1)
        scale = 1.0 / np.sqrt(HD)
        scores = jnp.einsum('bqhd,bkhd->bhqk', q, k) * scale
        scores = jnp.where(mask[None, None, :, :], scores, jnp.float32(-jnp.inf))
        probs = jax.nn.softmax(scores, axis=-1)
        o = jnp.einsum('bhqk,bkhd->bqhd', probs, v).reshape(b, s, h)
        return o @ Wo

    def _L0_xattn_ref(q, k, v):
        import jax, jax.numpy as jnp
        import numpy as np
        N_HEAD = 8
        b, d, m = q.shape
        c = v.shape[1]
        h = N_HEAD
        qh = q.reshape(b * h, d // h, m)
        kh = k.reshape(b * h, d // h, -1)
        vh = v.reshape(b * h, c // h, -1)
        scale = 1.0 / jnp.sqrt(jnp.asarray(d // h, dtype=q.dtype))
        qk = jnp.einsum('bdm,bdn->bmn', qh, kh) * scale
        sm = jax.nn.softmax(qk, axis=-1)
        ret = jnp.einsum('bmn,bcn->bcm', sm, vh)
        return ret.reshape(b, c, m)

    def _L0_ffn_ref(x, weight):
        import jax, jax.numpy as jnp
        import numpy as np
        BLOCK = 128
        MAXVAL = 448.0

        def _quant_dequant(x_flat):
            xb = x_flat.reshape(-1, BLOCK)
            s = jnp.max(jnp.abs(xb), axis=1, keepdims=True) / MAXVAL
            q = (xb / s).astype(jnp.float8_e4m3fn)
            return (q.astype(jnp.float32) * s).reshape(x_flat.shape)
        B, T, D = x.shape
        x_deq = _quant_dequant(x.reshape(-1)).reshape(B * T, D)
        w_deq = _quant_dequant(weight.reshape(-1)).reshape(weight.shape)
        out = x_deq @ w_deq.T
        return out.reshape(B, T, -1)
    x = _layernorm(x + _L0_attn_ref(x, L0_attn_Wqkv, L0_attn_q_norm_w, L0_attn_k_norm_w, L0_attn_Wo), axis=-1)
    x = _layernorm(x + _L0_xattn_ref(x, ctx_2048, ctx_2048), axis=-1)
    x = _layernorm(x + _L0_ffn_ref(x, L0_ffn_weight), axis=-1)
    return x

_drawn_inputs = setup_inputs


def setup_inputs(seed=0):
    import zlib

    import numpy as np

    out = dict(_drawn_inputs(seed))
    spreads = {'L0_attn_q_norm_w': (1.0, 0.2), 'L0_attn_k_norm_w': (1.0, 0.2)}
    factors = {}
    for name, (base, spread) in spreads.items():
        noise = np.random.default_rng([zlib.crc32(name.encode()), seed]).standard_normal(out[name].shape)
        drawn = base * np.exp(spread * noise) if base else spread * noise
        out[name] = jnp.asarray(drawn.astype(out[name].dtype))
    for name, factor in factors.items():
        out[name] = (out[name] * factor).astype(out[name].dtype)
    return out
```

```python
import concourse.bass as bass
from concourse import mybir
from contextlib import ExitStack


def post_ln_decoder_kernel(nc, x, ctx_in, wqkv, q_norm_w, k_norm_w, wo, wffn, cos_t, sin_t, out):
    F32, F32R = mybir.dt.float32, mybir.dt.float32r
    BF16, F16, I32 = mybir.dt.bfloat16, mybir.dt.float16, mybir.dt.int32
    ALU, ACT, AX = mybir.AluOpType, mybir.ActivationFunctionType, mybir.AxisListType

    BATCH, TOK, D = x.shape
    P = TOK
    NH, HD = 16, D // 16
    HH = HD // 2
    XH, XD = 8, TOK // 8
    KC = D // P
    HC = NH // KC
    GROUPS, GH = XH // 4, 4
    UNITS = GROUPS * KC
    SELF_SCALE, CROSS_SCALE = HD ** -0.5, XD ** -0.5
    WINDOW = 256
    assert TOK <= WINDOW
    RMS_EPS, LN_EPS = 1e-6, 1e-5
    QBLK, FP8_MAX = 128, 448.0
    NQ = D // QBLK
    SHIFT_UNIT = 64.0
    NEG = -1e30
    SROWS = 3 * HD
    XROWS = 96
    Q_PLANE, K_PLANE = (0, 0, 0, 1, 1), (0, 1, 2, 0, 1)
    QKV, SELF, MAX, CROSS, FFN = range(5)
    EXP_BITS = 0x7F800000
    MIN_NORMAL, MAGIC = 2.0 ** -6, 1.5 * 2.0 ** 20

    qpl_d = nc.dram_tensor("q_planes", [BATCH, 2, TOK, D], F16, kind="Internal").ap()
    kpl_d = nc.dram_tensor("k_planes", [BATCH, 3, TOK, D], BF16, kind="Internal").ap()
    x2_d = nc.dram_tensor("x2_rows", [BATCH, TOK, D], F32, kind="Internal").ap()
    sh1_d = nc.dram_tensor("self_shift", [BATCH, 2 * NH, TOK], F16, kind="Internal").ap()
    sh2_d = nc.dram_tensor("cross_shift", [BATCH, GROUPS, 32, P], F16, kind="Internal").ap()

    es = ExitStack()
    with es:
        def sb(name, shape, dt=F32):
            return es.enter_context(nc.sbuf_tensor(name, shape, dt))

        def bank(name):
            return es.enter_context(nc.psum_tensor(name, [P, 512], F32))

        def sem(name):
            return es.enter_context(nc.semaphore(name))

        w_h, w_l = sb("w_h", [P, KC, 3 * D], F32R), sb("w_l", [P, KC, 3 * D], F32R)
        wo_h, wo_l = sb("wo_h", [P, KC, D], F32R), sb("wo_l", [P, KC, D], F32R)
        wf_h, wf_l = sb("wf_h", [P, KC, D], F32R), sb("wf_l", [P, KC, D], F32R)
        cos_w = [sb(f"cos_w{i}", [P, NH, 2, HH]) for i in range(2)]
        sin_w = [sb(f"sin_w{i}", [P, NH, 2, HH]) for i in range(2)]
        cos_s, sin_s = sb("cos_s", [P, HH]), sb("sin_s", [P, HH])
        ident = sb("ident", [P, P])
        ident16 = sb("ident16", [P, P], F16)
        identb = sb("identb", [P, P], BF16)
        maskb = sb("maskb", [P, P], BF16)
        half = sb("half", [P, 1])
        xb = [sb(f"xb{i}", [P, D]) for i in range(2)]
        cx, cx_rest = sb("cx", [P, D]), sb("cx_rest", [P, D])
        lin_h, lin_l = sb("lin_h", [P, D], F32R), sb("lin_l", [P, D], F32R)
        ropeA, ropeB = sb("ropeA", [P, NH, 2, HH]), sb("ropeB", [P, NH, 2, HH])
        junk = sb("junk", [P, D], BF16)
        qkn = [sb(f"qkn{i}", [P, NH, 3, HD], F16) for i in range(2)]
        va = [sb(f"va{i}", [P, NH, HD + 1]) for i in range(2)]
        qs = sb("qs", [SROWS + 2, NH, P], F16)
        ks = sb("ks", [SROWS + 2, NH, P], F16)
        p1 = [sb(f"p1_{i}", [P, HC, P]) for i in range(2)]
        o1 = ropeB[:, :, :, :].rearrange("p h a d -> p (h a d)")
        x2, x2r = sb("x2", [P, D]), sb("x2r", [P, D])
        qpl = sb("qpl", [P, 2, D], F16)
        kpl = sb("kpl", [P, 3, D], BF16)
        qst = [sb(f"qst{i}", [XROWS + 2, XH, D], F16) for i in range(2)]
        kst = [sb(f"kst{i}", [XROWS + 2, XH, D], BF16) for i in range(2)]
        vT = [sb(f"vT{i}", [P, KC, XH, 2 * XD]) for i in range(2)]
        pp = sb("pp", [P, 2, GH, D])
        o2 = sb("o2", [P, GROUPS, D])
        x3 = sb("x3", [P, D])
        yq, yc = sb("yq", [P, D]), sb("yc", [P, D])
        o2n = yq[:].rearrange("p (c h d) -> p c h d", c=KC, h=XH)
        yout = sb("yout", [P, D])
        ssq, rms = sb("ssq", [P, 2]), sb("rms", [P, 2])
        nm1, sh1 = sb("nm1", [P, NH]), sb("sh1", [P, 2, NH], F16)
        sh1T = sb("sh1T", [2 * NH, P], F16)
        nm2, sh2 = sb("nm2", [P, GROUPS, 16]), sb("sh2", [P, GROUPS, 2, 16], F16)
        sh2T = [sb(f"sh2T{g}", [32, P], F16) for g in range(GROUPS)]
        r1 = sb("r1", [P, 2, NH // 2])
        st6 = [sb(f"st6_{i}", [P, 6]) for i in range(3)]
        mv = [sb(f"mv{i}", [P, 2]) for i in range(3)]
        rstd = [sb(f"rstd{i}", [P, 1]) for i in range(3)]
        r2 = sb("r2", [P, GROUPS, KC, GH])
        amax, qsc, qri = sb("amax", [P, NQ]), sb("qsc", [P, NQ]), sb("qri", [P, NQ])

        st = es.enter_context(nc.psum_tensor("st", [P, GH, 512], F32))
        pv = bank("pv")
        mx = bank("mx")
        bx = bank("bx")
        by = bank("by")

        d_setup = [sem(f"d_setup{i}") for i in range(2)]
        d_const = sem("d_const")
        d_x = [sem(f"d_x{i}") for i in range(2)]
        d_cx, d_kpl_stored = sem("d_cx"), sem("d_kpl_stored")
        d_x2_stored, d_x2r, d_qpl_stored = sem("d_x2_stored"), sem("d_x2r"), sem("d_qpl_stored")
        d_stack = [[sem(f"d_stack{i}{g}") for g in range(GROUPS)] for i in range(2)]
        d_sh1_stored, d_sh1 = sem("d_sh1_stored"), sem("d_sh1")
        d_sh2_stored = [sem(f"d_sh2_stored{g}") for g in range(GROUPS)]
        d_sh2 = [sem(f"d_sh2_{g}") for g in range(GROUPS)]
        d_out = sem("d_out")
        u_zero, u_const, u_dve = sem("u_zero"), sem("u_const"), sem("u_dve")
        u_staged, u_fT, u_done = sem("u_staged_used"), sem("u_ffn_transposed"), sem("u_done")
        bx_full, bx_free = sem("bx_full"), sem("bx_free")
        by_full, by_free = sem("by_full"), sem("by_free")
        mx_full, mx_free = sem("mx_full"), sem("mx_free")
        st_full, st_free = sem("st_full"), sem("st_free")
        pv_unit, pv_free = sem("pv_unit_done"), sem("pv_free")
        passed_sp, passed_pool, passed_dve = sem("passed_sp"), sem("passed_pool"), sem("passed_dve")
        s_xTh, s_oTh, s_xdh = sem("s_xT_high"), sem("s_oT_high"), sem("s_xdT_high")
        s_ssq, s_ms, s_rms = sem("s_ssq"), sem("s_mean_square"), sem("s_rms")
        s_rope, s_part_h, s_part_l = sem("s_rope"), sem("s_part_high"), sem("s_part_low")
        s_sc1, s_h1, s_sh1 = sem("s_shift1_scaled"), sem("s_shift1_high"), sem("s_shift1")
        s_sc2, s_h2, s_sh2 = sem("s_shift2_scaled"), sem("s_shift2_high"), sem("s_shift2")
        s_masked, s_r1, s_r2 = sem("s_masked"), sem("s_r1"), sem("s_r2")
        s_st6, s_mv, s_ve, s_rstd, s_ln = ([sem(f"s_{n}{i}") for i in range(3)]
                                           for n in ("st6_", "mv", "ve", "rstd", "ln"))
        s_qh, s_ql = sem("s_q_high"), sem("s_q_low")
        s_k1, s_kr, s_k2, s_k3 = sem("s_k1"), sem("s_k_rest"), sem("s_k2"), sem("s_k3")
        s_am, s_qsc, s_qri = sem("s_amax"), sem("s_qscale"), sem("s_qrecip")
        s_unit, s_exp, s_magic, s_sum, s_round, s_back = (
            sem(f"s_quant_{n}") for n in ("unit", "exp", "magic", "sum", "round", "back"))

        SLOTS = BATCH + FFN
        LOOP0 = FFN + 2
        ROUNDS = (BATCH - LOOP0) // 2 - 1

        class Count:

            def __init__(self, b, rnd):
                self.b, self.rnd, self.i = b, rnd, b % 2

            def idx(self, ahead=0):
                v = self.b + ahead
                return v if self.rnd is None else self.rnd * 2 + v

            def n(self, per, k):
                v = self.b * per + k
                return max(v, 0) if self.rnd is None else self.rnd * (2 * per) + v

            def n2(self, per, k):
                v = (self.b // 2) * per + k
                return v if self.rnd is None else self.rnd * per + v

        class Slot:
            def __init__(self, rep, rnd=None):
                self.rep, self.rnd = rep, rnd

            def at(self, stage):
                return Count(self.rep - stage, self.rnd)

            def has(self, stage):
                return 0 <= self.rep - stage < BATCH

        def run(eng, slot):
            for t in range(LOOP0):
                slot(Slot(t))
            with eng.Fori(0, ROUNDS) as rnd:
                for u in range(2):
                    slot(Slot(LOOP0 + u, rnd))
            for t in range(LOOP0 + 2 * ROUNDS, SLOTS):
                slot(Slot(t))

        X_TURNS = [("o2T", FFN, 0), ("o2T", FFN, 1), ("o2N", FFN, 0), ("xT", QKV, 0), ("q", QKV, 0),
                   ("k", QKV, 0), ("v", QKV, 0), ("xdT", FFN, 0), ("ffn", FFN, 0)]
        Y_TURNS = ([("vT", MAX, 0), ("tq", SELF, 0), ("tq", SELF, 1), ("tk", SELF, 0), ("tk", SELF, 1)]
                   + [("s1m", SELF, c) for c in range(KC)] + [("m1T", SELF, 0)]
                   + [("s1t", SELF, 0), ("s1t", SELF, 1), ("pv1", SELF, 0), ("mT", MAX, 0), ("s1t", SELF, 2),
                      ("s1t", SELF, 3), ("pv1", SELF, 1), ("oT", SELF, 0), ("wo", SELF, 0), ("mT", MAX, 1)])

        def turn(turns, s, name, k):
            def had(t):
                return [(n, kk) for n, stage, kk in turns if 0 <= t - stage < BATCH]
            v = sum(len(had(t)) for t in range(s.rep)) + had(s.rep).index((name, k))
            return v if s.rnd is None else s.rnd * (2 * len(turns)) + v

        def X(s, name, k=0):
            return turn(X_TURNS, s, name, k)

        def Y(s, name, k=0):
            return turn(Y_TURNS, s, name, k)

        U_CONST = 4 + 1 + 5 * 2 + 1

        block = es.enter_context(nc.Block())

        @block.sync
        def _(sp):
            sp.dma_start(cos_s[:], cos_t).then_inc(d_const, 16)
            sp.dma_start(sin_s[:], sin_t).then_inc(d_const, 16)
            for dst, w in ((ropeA, q_norm_w), (ropeB, k_norm_w)):
                sp.dma_start(dst[:].rearrange("p h a d -> p (h a d)"), w.partition_broadcast(P)).then_inc(d_const, 16)
            sp.dma_start(xb[0][:], x[0]).then_inc(d_x[0], 16)
            for n in range(3 * KC):
                if n >= 2:
                    sp.wait_ge(u_staged, n - 1)
                src = (wqkv, wo, wffn)[n // KC][(n % KC) * P:(n % KC + 1) * P, :]
                sp.dma_start(pp[:, n % 2].rearrange("p a d -> p (a d)")[:, 0:src.shape[1]], src)\
                  .then_inc(d_setup[n % 2], 16)
            sp.wait_ge(u_const, U_CONST)

            def load_stack(s, stage, g):
                b = s.at(stage)
                sp.wait_ge(d_qpl_stored, b.n(16, 16))
                sp.wait_ge(d_kpl_stored, b.n(16, 16))
                sp.sem_inc(passed_sp, 1)
                sp.wait_ge(pv_unit, b.n(UNITS, KC * (g + 1) - 2 * UNITS))
                sp.sem_inc(passed_sp, 1)
                for r in range(5):
                    for dst, src in ((qst, qpl_d[b.idx()][Q_PLANE[r]]), (kst, kpl_d[b.idx()][K_PLANE[r]])):
                        sp.dma_start(dst[b.i][r * XD:(r + 1) * XD, GH * g:GH * (g + 1), :],
                                     src[GH * g * XD:GH * (g + 1) * XD, :].rearrange("(h d) n -> d h n", d=XD))\
                          .then_inc(d_stack[b.i][g], 16)

            def load_shift(s, g):
                b = s.at(MAX)
                sp.wait_ge(by_free, Y(s, "mT", g) + 1)
                sp.sem_inc(passed_sp, 1)
                sp.dma_start(sh2_d[b.idx()][g], sh2T[g][:]).then_inc(d_sh2_stored[g], 16)
                sp.wait_ge(d_sh2_stored[g], b.n(16, 16))
                sp.sem_inc(passed_sp, 1)
                sp.dma_start(qst[b.i][XROWS:XROWS + 2, GH * g:GH * (g + 1), :]
                             .rearrange("a h (c m) -> a (h c) m", c=KC),
                             sh2_d[b.idx()][g].rearrange("(a r) m -> a r m", a=2)).then_inc(d_sh2[g], 16)

            def slot(s):
                if s.has(MAX):
                    load_stack(s, MAX, 1)
                if s.has(SELF):
                    b = s.at(SELF)
                    if s.has(MAX):
                        sp.wait_ge(by_full, Y(s, "vT") + 1)
                        sp.sem_inc(passed_sp, 1)
                    sp.wait_ge(s_kr, b.n(1, 0))
                    sp.sem_inc(passed_sp, 1)
                    sp.dma_start(cx[:], ctx_in[b.idx()]).then_inc(d_cx, 16)
                if s.has(CROSS):
                    b = s.at(CROSS)
                    if s.has(FFN):
                        sp.wait_ge(bx_free, X(s, "o2N") + 1)
                        sp.sem_inc(passed_sp, 1)
                    sp.wait_ge(d_x2_stored, b.n(16, 16))
                    sp.sem_inc(passed_sp, 1)
                    sp.dma_start(x2r[:], x2_d[b.idx()]).then_inc(d_x2r, 16)
                if s.has(SELF):
                    b = s.at(SELF)
                    sp.wait_ge(s_k3, b.n(1, 1))
                    sp.sem_inc(passed_sp, 1)
                    sp.dma_start(kpl_d[b.idx()].rearrange("g p n -> p g n"), kpl[:]).then_inc(d_kpl_stored, 16)
                    sp.wait_ge(by_free, Y(s, "m1T") + 1)
                    sp.sem_inc(passed_sp, 1)
                    sp.dma_start(sh1_d[b.idx()], sh1T[:]).then_inc(d_sh1_stored, 16)
                    sp.wait_ge(d_sh1_stored, b.n(16, 16))
                    sp.sem_inc(passed_sp, 1)
                    sp.dma_start(qs[SROWS:SROWS + 2, :, :],
                                 sh1_d[b.idx()].rearrange("(a h) q -> a h q", a=2)).then_inc(d_sh1, 16)
                if s.has(MAX):
                    load_shift(s, 0)
                if s.has(SELF):
                    b = s.at(SELF)
                    sp.wait_ge(by_free, Y(s, "wo") + 1)
                    sp.sem_inc(passed_sp, 1)
                if s.has(QKV) and s.rep + 1 < BATCH:
                    b = s.at(QKV)
                    sp.dma_start(xb[1 - b.i][:], x[b.idx(1)]).then_inc(d_x[1 - b.i], 16)
                if s.has(FFN):
                    b = s.at(FFN)
                    sp.wait_ge(s_ln[2], b.n(1, 1))
                    sp.sem_inc(passed_sp, 1)
                    sp.dma_start(out[b.idx()], yout[:]).then_inc(d_out, 16)
                if s.has(SELF):
                    b = s.at(SELF)
                    sp.wait_ge(s_ln[0], b.n(1, 1))
                    sp.sem_inc(passed_sp, 1)
                    sp.dma_start(x2_d[b.idx()], x2[:]).then_inc(d_x2_stored, 16)
                    sp.wait_ge(s_ql, b.n(1, 1))
                    sp.sem_inc(passed_sp, 1)
                    sp.dma_start(qpl_d[b.idx()].rearrange("g p n -> p g n"), qpl[:]).then_inc(d_qpl_stored, 16)
                    load_stack(s, SELF, 0)
                if s.has(MAX):
                    load_shift(s, 1)

            run(sp, slot)
            sp.wait_ge(d_out, 16 * BATCH)



        @block.gpsimd
        def _(pool):
            g_ = nc.gpsimd
            for m in (ident, ident16, identb, maskb):
                g_.memset(m[:], 0.0).then_inc(u_zero, 1)
            pool.wait_ge(u_zero, 4)
            for m in (ident, ident16, identb):
                g_.affine_select(out=m[:], in_=m[:], compare_op=ALU.not_equal, fill=1.0, base=0,
                                 pattern=[[-1, P]], channel_multiplier=1).then_inc(u_const, 1)
            g_.affine_select(out=maskb[:], in_=maskb[:], compare_op=ALU.is_ge, fill=NEG, base=0,
                             pattern=[[-1, P]], channel_multiplier=1).then_inc(u_const, 1)
            g_.memset(half[:], -0.5).then_inc(u_const, 1)
            n = 5
            for rows, value in [r for i in range(2) for r in (
                    (va[i][:, :, HD:HD + 1], 1.0), (vT[i][:, :, :, XD:2 * XD], 1.0),
                    (qst[i][64:XROWS, :, :], 0.0), (kst[i][64:XROWS, :, :], 0.0),
                    (kst[i][XROWS:XROWS + 2, :, :], SHIFT_UNIT))] + [(ks[SROWS:SROWS + 2, :, :], SHIFT_UNIT)]:
                pool.wait_ge(u_const, n)
                g_.memset(rows, value).then_inc(u_const, 1)
                n += 1
            pool.wait_ge(u_const, U_CONST)
            pool.wait_ge(u_done, 1)

            def mean_square(s, k):
                b = s.at(QKV)
                pool.wait_ge(s_ssq, b.n(2, k + 1))
                pool.sem_inc(passed_pool, 1)
                g_.tensor_scalar(rms[:, k:k + 1], ssq[:, k:k + 1], 1.0 / D, RMS_EPS, ALU.mult, ALU.add)\
                  .then_inc(s_ms, 1)
                pool.wait_ge(s_ms, b.n(2, k + 1))
                g_.tensor_tensor(rms[:, k:k + 1], rms[:, k:k + 1], half[:], ALU.pow).then_inc(s_rms, 1)

            def layer_rstd(s, i):
                b = s.at((SELF, FFN, FFN)[i])
                pool.wait_ge(s_mv[i], b.n(1, 1))
                pool.sem_inc(passed_pool, 1)
                g_.tensor_scalar(rstd[i][:], mv[i][:, 1:2], 1.0, LN_EPS, ALU.mult, ALU.add).then_inc(s_ve[i], 1)
                pool.wait_ge(s_ve[i], b.n(1, 1))
                g_.tensor_tensor(rstd[i][:], rstd[i][:], half[:], ALU.pow).then_inc(s_rstd[i], 1)

            def rope_sum(s, k):
                b = s.at(QKV)
                pool.wait_ge(bx_free, X(s, ("q", "k")[k]) + 1)
                g_.tensor_tensor(ropeA[:], ropeA[:], ropeB[:], ALU.add).then_inc(s_rope, 1)
                pool.wait_ge(s_part_h, b.n(2, k + 1))
                g_.tensor_tensor(qkn[k][:, :, 2 - k, :], ropeA[:].rearrange("p h a d -> p h (a d)"),
                                 qkn[k][:, :, 0, :], ALU.subtract).then_inc(s_part_l, 1)

            def mask(s, c):
                b = s.at(SELF)
                pool.wait_ge(by_free, Y(s, "s1t", c) + 1)
                pool.sem_inc(passed_pool, 1)
                g_.affine_select(out=p1[c % 2][:], in_=p1[c % 2][:], compare_op=ALU.is_ge, fill=0.0, base=0,
                                 pattern=[[0, HC], [1, P]], channel_multiplier=-1).then_inc(s_masked, 1)

            def context_rest(s, k):
                b = s.at(SELF)
                if k == 0:
                    pool.wait_ge(s_k1, b.n(1, 1))
                    g_.tensor_tensor(cx_rest[:], cx[:], kpl[:, 0, :], ALU.subtract).then_inc(s_kr, 1)
                else:
                    pool.wait_ge(s_k2, b.n(1, 1))
                    g_.tensor_tensor(kpl[:, 2, :], cx_rest[:], kpl[:, 1, :], ALU.subtract).then_inc(s_k3, 1)

            def quantise(s, step):
                b = s.at(FFN)
                v = yq[:].rearrange("p (n k) -> p n k", n=NQ)
                if step == 0:
                    pool.wait_ge(s_qri, b.n(1, 1))
                    g_.tensor_tensor(v, x3[:].rearrange("p (n k) -> p n k", n=NQ),
                                     qri[:].unsqueeze(2).to_broadcast([P, NQ, QBLK]), ALU.mult).then_inc(s_unit, 1)
                else:
                    pool.wait_ge(s_magic, b.n(1, 1))
                    g_.tensor_tensor(yq[:], yq[:], yc[:], ALU.add).then_inc(s_sum, 1)
                    pool.wait_ge(s_sum, b.n(1, 1))
                    g_.tensor_tensor(yq[:], yq[:], yc[:], ALU.subtract).then_inc(s_round, 1)
                    pool.wait_ge(s_round, b.n(1, 1))
                    g_.tensor_tensor(v, v, qsc[:].unsqueeze(2).to_broadcast([P, NQ, QBLK]), ALU.mult)\
                      .then_inc(s_back, 1)

            def query_low(s, _):
                b = s.at(SELF)
                pool.wait_ge(s_qh, b.n(1, 1))
                g_.tensor_tensor(qpl[:, 1, :], x2[:], qpl[:, 0, :], ALU.subtract).then_inc(s_ql, 1)

            ORDER = [(context_rest, SELF, 0), (context_rest, SELF, 1), (layer_rstd, FFN, 1),
                     (mean_square, QKV, 0), (rope_sum, QKV, 0), (quantise, FFN, 0), (mean_square, QKV, 1),
                     (rope_sum, QKV, 1), (quantise, FFN, 1), (mask, SELF, 0), (mask, SELF, 1), (mask, SELF, 2),
                     (mask, SELF, 3), (layer_rstd, FFN, 2), (layer_rstd, SELF, 0), (query_low, SELF, 0)]

            def slot(s):
                for piece, stage, k in ORDER:
                    if s.has(stage):
                        piece(s, k)

            run(pool, slot)

        @block.scalar
        def _(act):
            a = nc.scalar
            act.wait_ge(u_done, 1)
            act.wait_ge(u_const, U_CONST)

            def probs(s, m):
                b = s.at(CROSS)
                unit, j = m // 2, 2 * (m % 2)
                act.wait_ge(st_full, b.n(2 * UNITS, m + 1))
                act.wait_ge(pv_unit, b.n(UNITS, unit - 1))
                a.activation(pp[:, unit % 2, j:j + 2, :], st[:, j:j + 2, :], ACT.Exp, scale=CROSS_SCALE)\
                 .then_inc(st_free, 1)

            def group_out(s, g):
                b = s.at(CROSS)
                act.wait_ge(pv_unit, b.n(UNITS, KC * (g + 1)))
                if s.has(FFN):
                    act.wait_ge(bx_full, X(s, "o2T", g) + 1)
                a.activation(o2[:, g, :], pv[:], ACT.Copy).then_inc(pv_free, 1)

            def xT_high(s, _):
                act.wait_ge(bx_full, X(s, "xT") + 1)
                a.activation(lin_h[:], bx[:], ACT.Copy).then_inc(s_xTh, 1)

            def square(s, k):
                b = s.at(QKV)
                act.wait_ge(bx_full, X(s, ("q", "k")[k]) + 1)
                act.wait_ge(s_ms, b.n(2, k - 1))
                a.activation(junk[:], bx[:], ACT.Square, accum_out=ssq[:, k:k + 1]).then_inc(s_ssq, 1)

            def part_high(s, k):
                b = s.at(QKV)
                act.wait_ge(s_rope, b.n(2, k + 1))
                if s.has(SELF):
                    act.wait_ge(by_full, Y(s, ("tq", "tk")[k], 1) + 1)
                src = ropeA[:].rearrange("p h a d -> p h (a d)")
                a.activation(qkn[k][:, :, 0, :], src, ACT.Copy)
                a.activation(qkn[k][:, :, 1 + k, :], src, ACT.Copy).then_inc(s_part_h, 1)

            def value(s, _):
                b = s.at(QKV)
                act.wait_ge(bx_full, X(s, "v") + 1)
                a.activation(va[b.i][:, :, 0:HD], bx[:].rearrange("p (h d) -> p h d", h=NH), ACT.Copy)\
                 .then_inc(bx_free, 1)

            def self_stack(s, i):
                act.wait_ge(by_full, Y(s, ("tq", "tk")[i // 2], i % 2) + 1)
                dst = (qs, ks)[i // 2][0:SROWS, 8 * (i % 2):8 * (i % 2) + 8, :]
                a.activation(dst, by[0:SROWS, :].bitcast(F16).rearrange("p (h t) -> p h t", h=8), ACT.Copy)\
                 .then_inc(by_free, 1)

            def self_shift_T(s, _):
                b = s.at(SELF)
                act.wait_ge(by_full, Y(s, "m1T") + 1)
                act.wait_ge(d_sh1_stored, b.n(16, 0))
                a.activation(sh1T[:], by[0:2 * NH, 0:P // 2].bitcast(F16), ACT.Copy).then_inc(by_free, 1)

            def self_probs(s, c):
                act.wait_ge(by_full, Y(s, "s1t", c) + 1)
                a.activation(p1[c % 2][:], by[:].rearrange("p (h q) -> p h q", h=HC), ACT.Exp, scale=SELF_SCALE)\
                 .then_inc(by_free, 1)

            def oT_high(s, _):
                act.wait_ge(by_full, Y(s, "oT") + 1)
                a.activation(lin_h[:], by[:], ACT.Copy).then_inc(s_oTh, 1)

            def query_high(s, _):
                b = s.at(SELF)
                act.wait_ge(s_ln[0], b.n(1, 1))
                act.wait_ge(d_qpl_stored, b.n(16, 0))
                a.activation(qpl[:, 0, :], x2[:], ACT.Copy).then_inc(s_qh, 1)

            def context_high(s, k):
                b = s.at(SELF)
                if k == 0:
                    act.wait_ge(d_cx, b.n(16, 16))
                    act.wait_ge(d_kpl_stored, b.n(16, 0))
                    a.activation(kpl[:, 0, :], cx[:], ACT.Copy).then_inc(s_k1, 1)
                else:
                    act.wait_ge(s_kr, b.n(1, 1))
                    a.activation(kpl[:, 1, :], cx_rest[:], ACT.Copy).then_inc(s_k2, 1)

            def context_T(s, _):
                b = s.at(MAX)
                act.wait_ge(by_full, Y(s, "vT") + 1)
                a.activation(vT[b.i][:, :, :, 0:XD], by[:].rearrange("p (i h d) -> p i h d", i=KC, h=XH),
                             ACT.Copy).then_inc(by_free, 1)

            def cross_shift_T(s, g):
                b = s.at(MAX)
                act.wait_ge(by_full, Y(s, "mT", g) + 1)
                act.wait_ge(d_sh2_stored[g], b.n(16, 0))
                a.activation(sh2T[g][:], by[0:32, 0:P // 2].bitcast(F16), ACT.Copy).then_inc(by_free, 1)

            def xdT_high(s, _):
                act.wait_ge(bx_full, X(s, "xdT") + 1)
                a.activation(lin_h[:], bx[:], ACT.Copy).then_inc(s_xdh, 1)

            BETWEEN = {
                0: [(context_T, MAX, 0), (self_stack, SELF, 0)],
                1: [(self_stack, SELF, 1), (self_stack, SELF, 2)],
                2: [(self_stack, SELF, 3), (xT_high, QKV, 0), (context_high, SELF, 0)],
                3: [(context_high, SELF, 1)],
                4: [(square, QKV, 0)],
                5: [(self_shift_T, SELF, 0)],
                6: [(part_high, QKV, 0), (square, QKV, 1)],
                7: [(self_probs, SELF, 0)],
                8: [(self_probs, SELF, 1), (part_high, QKV, 1)],
                9: [(value, QKV, 0), (cross_shift_T, MAX, 0), (self_probs, SELF, 2), (xdT_high, FFN, 0)],
                10: [(self_probs, SELF, 3)], 11: [(group_out, CROSS, 0)],
                12: [(oT_high, SELF, 0)],
                15: [(query_high, SELF, 0)],
                16: [(group_out, CROSS, 1), (cross_shift_T, MAX, 1)],
            }

            def slot(s):
                for m in range(2 * UNITS + 1):
                    for piece, stage, k in BETWEEN.get(m, ()):
                        if s.has(stage):
                            piece(s, k)
                    if s.has(CROSS) and m < 2 * UNITS:
                        probs(s, m)

            run(act, slot)

        @block.vector
        def _(dve):
            v = nc.vector
            done = [0]

            def step(ins):
                done[0] += 1
                ins.then_inc(u_dve, 1)
                dve.wait_ge(u_dve, done[0])

            dve.wait_ge(d_const, 64)
            for i, w in enumerate((ropeA, ropeB)):
                v.tensor_tensor(cos_w[i][:], w[:], cos_s[:].unsqueeze(1).unsqueeze(1).to_broadcast([P, NH, 2, HH]),
                                ALU.mult)
                sin_b = sin_s[:].unsqueeze(1).to_broadcast([P, NH, HH])
                v.scalar_tensor_tensor(sin_w[i][:, :, 0, :], w[:, :, 1, :], -1.0, sin_b, ALU.mult, ALU.mult)
                step(v.tensor_tensor(sin_w[i][:, :, 1, :], w[:, :, 0, :], sin_b, ALU.mult))
            for n in range(3 * KC):
                c, piece = n % KC, pp[:, n % 2].rearrange("p a d -> p (a d)")
                dve.wait_ge(d_setup[n % 2], 16 * (n // 2 + 1))
                if n < 2 * KC:
                    hi, lo = ((w_h, w_l), (wo_h, wo_l))[n // KC]
                    src = piece[:, 0:hi.shape[2]]
                    step(v.tensor_copy(hi[:, c, :], src))
                    v.tensor_tensor(lo[:, c, :], src, hi[:, c, :].bitcast(F32), ALU.subtract).then_inc(u_staged, 1)
                    continue
                src = piece[:, 0:D].rearrange("p (n k) -> p n k", n=NQ)
                y3 = yq[:].rearrange("p (n k) -> p n k", n=NQ)
                if c:
                    dve.wait_ge(u_fT, c)
                step(v.tensor_reduce(amax[:], src, AX.X, ALU.max, apply_absolute_value=True))
                step(v.tensor_scalar(qsc[:], amax[:], 1.0 / FP8_MAX, None, ALU.mult))
                step(v.reciprocal(qri[:], qsc[:]))
                step(v.tensor_tensor(y3, src, qri[:].unsqueeze(2).to_broadcast([P, NQ, QBLK]), ALU.mult))
                step(v.tensor_scalar(yc[:].bitcast(I32), yq[:].bitcast(I32), EXP_BITS, None, ALU.bitwise_and))
                step(v.tensor_scalar(yc[:], yc[:], MIN_NORMAL, MAGIC, ALU.max, ALU.mult))
                step(v.tensor_tensor(yq[:], yq[:], yc[:], ALU.add))
                step(v.tensor_tensor(yq[:], yq[:], yc[:], ALU.subtract))
                v.tensor_tensor(y3, y3, qsc[:].unsqueeze(2).to_broadcast([P, NQ, QBLK]), ALU.mult)\
                 .then_inc(u_staged, 1)
                dve.wait_ge(u_fT, c + 1)
                t4 = mx[:].rearrange("p (k o) -> p k o", k=KC)
                cols = slice(c * P, (c + 1) * P)
                step(v.tensor_copy(wf_h[:, :, cols], t4))
                step(v.tensor_tensor(wf_l[:, :, cols], t4, wf_h[:, :, cols].bitcast(F32), ALU.subtract))
            v.memset(r1[:], 0.0).then_inc(u_done, 1)
            dve.wait_ge(u_done, 1)

            def cross_max(s, n):
                b = s.at(MAX)
                h, c = n // KC, n % KC
                at = (h % GH) * KC + c
                dve.wait_ge(mx_full, b.n(XH * KC, n + 1))
                v.tensor_reduce(nm2[:, h // GH, at:at + 1], mx[:], AX.X, ALU.max, negate=True).then_inc(mx_free, 1)

            def split_shift(maxima, parts, unit, counts, per, k, b):
                scaled, high, low = counts
                v.tensor_scalar(maxima, maxima, 1.0 / SHIFT_UNIT, None, ALU.mult).then_inc(scaled, 1)
                dve.wait_ge(scaled, b.n(per, k + 1))
                v.tensor_copy(parts[0], maxima).then_inc(high, 1)
                dve.wait_ge(high, b.n(per, k + 1))
                v.tensor_tensor(parts[1], maxima, parts[0], ALU.subtract).then_inc(low, 1)

            def cross_shift(s, g):
                b = s.at(MAX)
                dve.wait_ge(mx_free, b.n(XH * KC, 16 * (g + 1)))
                split_shift(nm2[:, g, :], (sh2[:, g, 0, :], sh2[:, g, 1, :]), None, (s_sc2, s_h2, s_sh2), GROUPS, g, b)

            def self_max(s, c):
                dve.wait_ge(by_full, Y(s, "s1m", c) + 1)
                v.tensor_reduce(nm1[:, HC * c:HC * (c + 1)], by[:].rearrange("p (h k) -> p h k", h=HC), AX.X,
                                ALU.max, negate=True).then_inc(by_free, 1)

            def self_shift(s, _):
                b = s.at(SELF)
                dve.wait_ge(by_free, Y(s, "s1m", KC - 1) + 1)
                split_shift(nm1[:], (sh1[:, 0, :], sh1[:, 1, :]), None, (s_sc1, s_h1, s_sh1), 1, 0, b)

            def xT_low(s, _):
                b = s.at(QKV)
                dve.wait_ge(s_xTh, b.n(1, 1))
                v.tensor_tensor(lin_l[:], bx[:], lin_h[:].bitcast(F32), ALU.subtract).then_inc(bx_free, 1)

            def rope_terms(s, k):
                b = s.at(QKV)
                dve.wait_ge(s_rms, b.n(2, k + 1))
                dve.wait_ge(s_part_l, b.n(2, k))
                if k == 0 and s.has(MAX):
                    dve.wait_ge(by_full, Y(s, "tq", 0) + 1)
                src = bx[:].rearrange("p (h a d) -> p h a d", h=NH, a=2)
                v.scalar_tensor_tensor(ropeA[:].rearrange("p h a d -> p (h a d)"), bx[:], rms[:, k:k + 1],
                                       cos_w[k][:].rearrange("p h a d -> p (h a d)"), ALU.mult, ALU.mult)
                v.scalar_tensor_tensor(ropeB[:, :, 0, :], src[:, :, 1, :], rms[:, k:k + 1], sin_w[k][:, :, 0, :],
                                       ALU.mult, ALU.mult)
                v.scalar_tensor_tensor(ropeB[:, :, 1, :], src[:, :, 0, :], rms[:, k:k + 1], sin_w[k][:, :, 1, :],
                                       ALU.mult, ALU.mult).then_inc(bx_free, 1)

            def self_norm(s, i):
                b = s.at(SELF)
                dve.wait_ge(by_full, Y(s, "pv1", i) + 1)
                src = by[:, 0:8 * (HD + 1)].rearrange("p (h d) -> p h d", h=8)
                v.reciprocal(r1[:, i, :].unsqueeze(2), src[:, :, HD:HD + 1]).then_inc(s_r1, 1)
                dve.wait_ge(s_r1, b.n(2, i + 1))
                if s.has(QKV):
                    dve.wait_ge(s_rope, s.at(QKV).n(2, 2))
                v.tensor_tensor(o1[:, 8 * HD * i:8 * HD * (i + 1)].rearrange("p (h d) -> p h d", h=8),
                                src[:, :, 0:HD], r1[:, i, :].unsqueeze(2).to_broadcast([P, 8, HD]), ALU.mult)\
                 .then_inc(by_free, 1)

            def oT_low(s, _):
                b = s.at(SELF)
                dve.wait_ge(s_oTh, b.n(1, 1))
                v.tensor_tensor(lin_l[:], by[:], lin_h[:].bitcast(F32), ALU.subtract).then_inc(by_free, 1)

            def layernorm_stats(s, i, rows, ready, value):
                b = s.at((SELF, FFN, FFN)[i])
                dve.wait_ge(ready, value)
                v.bn_stats(st6[i][:], rows[:]).then_inc(s_st6[i], 1)
                dve.wait_ge(s_st6[i], b.n(1, 1))
                dve.sem_inc(passed_dve, 1)
                v.bn_aggr(mv[i][:], st6[i][:]).then_inc(s_mv[i], 1)

            def layernorm(s, i):
                b = s.at((SELF, FFN, FFN)[i])
                rows = (x2, x3, yout)[i]
                dve.wait_ge(s_rstd[i], b.n(1, 1))
                v.tensor_scalar(rows[:], rows[:], mv[i][:, 0:1], rstd[i][:], ALU.subtract, ALU.mult)\
                 .then_inc(s_ln[i], 1)

            def add_self(s, _):
                b = s.at(SELF)
                dve.wait_ge(by_full, Y(s, "wo") + 1)
                dve.wait_ge(d_x2_stored, b.n(16, 0))
                dve.wait_ge(s_ql, b.n(1, 0))
                v.tensor_tensor(x2[:], by[:], xb[b.i][:], ALU.add).then_inc(by_free, 1)
                layernorm_stats(s, 0, x2, by_free, Y(s, "wo") + 1)

            def cross_norm(s, g):
                b = s.at(FFN)
                dve.wait_ge(bx_full, X(s, "o2T", g) + 1)
                src = bx[:].rearrange("p (c j d) -> p c j d", c=KC, j=GH)
                v.reciprocal(r2[:, g].unsqueeze(3), src[:, :, :, XD:XD + 1]).then_inc(s_r2, 1)
                dve.wait_ge(s_r2, b.n(GROUPS, g + 1))
                v.tensor_tensor(o2n[:, :, GH * g:GH * (g + 1), :], src[:, :, :, 0:XD],
                                r2[:, g].unsqueeze(3).to_broadcast([P, KC, GH, XD]), ALU.mult).then_inc(bx_free, 1)

            def add_cross(s, _):
                b = s.at(FFN)
                dve.wait_ge(bx_full, X(s, "o2N") + 1)
                dve.wait_ge(d_x2r, b.n(16, 16))
                v.tensor_tensor(x3[:], bx[:], x2r[:], ALU.add).then_inc(bx_free, 1)
                layernorm_stats(s, 1, x3, bx_free, X(s, "o2N") + 1)

            def quant_scale(s, _):
                b = s.at(FFN)
                dve.wait_ge(s_ln[1], b.n(1, 1))
                v.tensor_reduce(amax[:], x3[:].rearrange("p (n k) -> p n k", n=NQ), AX.X, ALU.max,
                                apply_absolute_value=True).then_inc(s_am, 1)
                dve.wait_ge(s_am, b.n(1, 1))
                v.tensor_scalar(qsc[:], amax[:], 1.0 / FP8_MAX, None, ALU.mult).then_inc(s_qsc, 1)
                dve.wait_ge(s_qsc, b.n(1, 1))
                v.reciprocal(qri[:], qsc[:]).then_inc(s_qri, 1)

            def quant_magic(s, _):
                b = s.at(FFN)
                dve.wait_ge(s_unit, b.n(1, 1))
                v.tensor_scalar(yc[:].bitcast(I32), yq[:].bitcast(I32), EXP_BITS, None, ALU.bitwise_and)\
                 .then_inc(s_exp, 1)
                dve.wait_ge(s_exp, b.n(1, 1))
                v.tensor_scalar(yc[:], yc[:], MIN_NORMAL, MAGIC, ALU.max, ALU.mult).then_inc(s_magic, 1)

            def xdT_low(s, _):
                b = s.at(FFN)
                dve.wait_ge(s_xdh, b.n(1, 1))
                v.tensor_tensor(lin_l[:], bx[:], lin_h[:].bitcast(F32), ALU.subtract).then_inc(bx_free, 1)

            def add_ffn(s, _):
                b = s.at(FFN)
                dve.wait_ge(bx_full, X(s, "ffn") + 1)
                dve.wait_ge(d_out, b.n(16, 0))
                v.tensor_tensor(yout[:], bx[:], x3[:], ALU.add).then_inc(bx_free, 1)
                layernorm_stats(s, 2, yout, bx_free, X(s, "ffn") + 1)

            BETWEEN = {
                1: [(cross_norm, FFN, 0), (cross_norm, FFN, 1)],
                3: [(add_cross, FFN, 0)], 4: [(xT_low, QKV, 0)],
                5: [(self_max, SELF, 0), (layernorm, FFN, 1), (quant_scale, FFN, 0)],
                6: [(self_max, SELF, 1)], 7: [(self_max, SELF, 2)],
                8: [(self_max, SELF, 3), (self_shift, SELF, 0), (rope_terms, QKV, 0)],
                11: [(quant_magic, FFN, 0)],
                13: [(rope_terms, QKV, 1)],
                16: [(cross_shift, MAX, 0)], 17: [(self_norm, SELF, 0)],
                19: [(xdT_low, FFN, 0)], 22: [(self_norm, SELF, 1)],
                23: [(add_ffn, FFN, 0)], 24: [(oT_low, SELF, 0)], 26: [(layernorm, FFN, 2)],
                28: [(add_self, SELF, 0)], 30: [(layernorm, SELF, 0)],
                32: [(cross_shift, MAX, 1)],
            }

            def slot(s):
                for n in range(XH * KC + 1):
                    for piece, stage, k in BETWEEN.get(n, ()):
                        if s.has(stage):
                            piece(s, k)
                    if s.has(MAX) and n < XH * KC:
                        cross_max(s, n)

            run(dve, slot)

        @block.tensor
        def _(pe):
            t = nc.tensor
            pe.wait_ge(u_const, U_CONST)
            for c in range(KC):
                pe.wait_ge(u_staged, 2 * KC + c + 1)
                for k in range(KC):
                    last = t.transpose(mx[:, k * P:(k + 1) * P], yq[:, k * P:(k + 1) * P], ident[:])
                last.then_inc(u_fT, 1)
            pe.wait_ge(u_done, 1)

            def blocks(dst, src, idm=ident):
                for c in range(KC):
                    last = t.transpose(dst[:, c * P:(c + 1) * P], src(c), idm[:])
                return last

            def linear(dst, wh, wl, cols, part, parts=3):
                for c in range(KC):
                    if c * parts // KC != part and parts > 1:
                        continue
                    rows = slice(c * P, (c + 1) * P)
                    for i, (a, w) in enumerate(((lin_h, wh), (lin_h, wl), (lin_l, wh))):
                        last = t.matmul(dst[:], a[:, rows], w[:, c, cols], start=(c == 0 and i == 0),
                                        stop=(c == KC - 1 and i == 2))
                return last

            def proj(s, which, part):
                b = s.at(QKV)
                name = ("q", "k", "v")[which]
                if part == 0:
                    pe.wait_ge(bx_free, X(s, name))
                last = linear(bx, w_h, w_l, slice(which * D, (which + 1) * D), part, KC)
                if part == KC - 1:
                    last.then_inc(bx_full, 1)

            def proj_q(s, part):
                proj(s, 0, part)

            def proj_k(s, part):
                proj(s, 1, part)

            def proj_v(s, part):
                proj(s, 2, part)

            def x_T(s, _):
                b = s.at(QKV)
                pe.wait_ge(d_x[b.i], b.n2(16, 16))
                pe.wait_ge(bx_free, X(s, "xT"))
                blocks(bx, lambda c: xb[b.i][:, c * P:(c + 1) * P]).then_inc(bx_full, 1)

            def parts_T(s, i):
                b = s.at(SELF)
                k = i // 2
                pe.wait_ge(s_part_l, b.n(2, k + 1))
                pe.wait_ge(by_free, Y(s, ("tq", "tk")[k], i % 2))
                for h in range(8):
                    last = t.transpose(by[0:SROWS, h * P // 2:(h + 1) * P // 2].bitcast(F16),
                                       qkn[k][:, 8 * (i % 2) + h, :, :].rearrange("p g d -> p (g d)"), ident16[:])
                last.then_inc(by_full, 1)

            def self_scores(s, c):
                pe.wait_ge(by_free, Y(s, "s1m", c))
                t.matmul(by[:].rearrange("p (h k) -> p h k", h=HC), identb[:], maskb[:].unsqueeze(1).to_broadcast([P, HC, P]), start=True, stop=False)
                for j in range(HC):
                    last = t.matmul(by[:, j * P:(j + 1) * P], qs[0:SROWS, HC * c + j, :], ks[0:SROWS, HC * c + j, :],
                                    start=False, stop=(j == HC - 1))
                last.then_inc(by_full, 1)

            def self_shift_T(s, _):
                b = s.at(SELF)
                pe.wait_ge(s_sh1, b.n(1, 1))
                pe.wait_ge(by_free, Y(s, "m1T"))
                t.transpose(by[0:2 * NH, 0:P // 2].bitcast(F16), sh1[:].rearrange("p a h -> p (a h)"), ident16[:])\
                 .then_inc(by_full, 1)

            def self_scores_T(s, c):
                b = s.at(SELF)
                pe.wait_ge(d_sh1, b.n(16, 16))
                pe.wait_ge(by_free, Y(s, "s1t", c))
                for j in range(HC):
                    last = t.matmul(by[:, j * P:(j + 1) * P], ks[:, HC * c + j, :], qs[:, HC * c + j, :],
                                    start=True, stop=True)
                last.then_inc(by_full, 1)

            def self_pv(s, i):
                b = s.at(SELF)
                pe.wait_ge(s_masked, b.n(KC, 2 * i + 2))
                pe.wait_ge(by_free, Y(s, "pv1", i))
                for h in range(8):
                    last = t.matmul(by[:, h * (HD + 1):(h + 1) * (HD + 1)], p1[h // HC][:, h % HC, :],
                                    va[b.i][:, 8 * i + h, :], start=True, stop=True)
                last.then_inc(by_full, 1)

            def o_T(s, _):
                pe.wait_ge(by_free, Y(s, "oT"))
                blocks(by, lambda c: o1[:, c * P:(c + 1) * P]).then_inc(by_full, 1)

            def proj_o(s, part):
                if part == 0:
                    pe.wait_ge(by_free, Y(s, "wo"))
                last = linear(by, wo_h, wo_l, slice(0, D), part, KC)
                if part == KC - 1:
                    last.then_inc(by_full, 1)

            def context_T(s, _):
                b = s.at(MAX)
                pe.wait_ge(d_cx, b.n(16, 16))
                pe.wait_ge(by_free, Y(s, "vT"))
                blocks(by, lambda c: cx[:, c * P:(c + 1) * P]).then_inc(by_full, 1)

            def cross_scores(s, n):
                b = s.at(MAX)
                h, c = n // KC, n % KC
                if n % (GH * KC) == 0:
                    pe.wait_ge(d_stack[b.i][h // GH], b.n2(160, 160))
                pe.wait_ge(mx_free, b.n(XH * KC, n))
                t.matmul(mx[:], qst[b.i][0:XROWS, h, c * P:(c + 1) * P], kst[b.i][0:XROWS, h, :],
                         start=True, stop=True).then_inc(mx_full, 1)

            def cross_shift_T(s, g):
                b = s.at(MAX)
                pe.wait_ge(s_sh2, b.n(GROUPS, g + 1))
                pe.wait_ge(by_free, Y(s, "mT", g))
                t.transpose(by[0:32, 0:P // 2].bitcast(F16), sh2[:, g].rearrange("p a h -> p (a h)"), ident16[:])\
                 .then_inc(by_full, 1)

            def cross_scores_T(s, m):
                b = s.at(CROSS)
                g, i = m // 2 // KC, m // 2 % KC
                if m % (2 * KC) == 0:
                    pe.wait_ge(d_sh2[g], b.n(16, 16))
                pe.wait_ge(st_free, b.n(2 * UNITS, m - 1))
                for j in (2 * (m % 2), 2 * (m % 2) + 1):
                    h = GH * g + j
                    last = t.matmul(st[:, j, :], kst[b.i][:, h, i * P:(i + 1) * P], qst[b.i][:, h, :],
                                    start=True, stop=True)
                last.then_inc(st_full, 1)

            def cross_pv(s, unit):
                b = s.at(CROSS)
                g, i = unit // KC, unit % KC
                pe.wait_ge(st_free, b.n(2 * UNITS, 2 * unit + 2))
                if i == 0:
                    pe.wait_ge(pv_free, b.n(GROUPS, g))
                for j in range(GH):
                    last = t.matmul(pv[32 * j:32 * j + 2 * XD, :], vT[b.i][:, i, GH * g + j, :],
                                    pp[:, unit % 2, j, :], start=(i == 0), stop=(i == KC - 1))
                last.then_inc(pv_unit, 1)

            def group_T(s, g):
                b = s.at(FFN)
                pe.wait_ge(pv_free, b.n(GROUPS, g + 1))
                pe.wait_ge(bx_free, X(s, "o2T", g))
                blocks(bx, lambda c: o2[:, g, c * P:(c + 1) * P]).then_inc(bx_full, 1)

            def back_T(s, _):
                pe.wait_ge(bx_free, X(s, "o2N"))
                blocks(bx, lambda c: o2n[:, c].rearrange("p h d -> p (h d)")).then_inc(bx_full, 1)

            def quant_T(s, _):
                b = s.at(FFN)
                pe.wait_ge(s_back, b.n(1, 1))
                pe.wait_ge(bx_free, X(s, "xdT"))
                blocks(bx, lambda c: yq[:, c * P:(c + 1) * P]).then_inc(bx_full, 1)

            def ffn(s, part):
                if part == 0:
                    pe.wait_ge(bx_free, X(s, "ffn"))
                last = linear(bx, wf_h, wf_l, slice(0, D), part, KC)
                if part == KC - 1:
                    last.then_inc(bx_full, 1)

            BETWEEN = {
                0: [(context_T, MAX, 0), (parts_T, SELF, 0), (group_T, FFN, 0)],
                1: [(parts_T, SELF, 1), (group_T, FFN, 1)],
                2: [(parts_T, SELF, 2), (back_T, FFN, 0)],
                3: [(parts_T, SELF, 3), (x_T, QKV, 0)],
                4: [(self_scores, SELF, 0), (proj_q, QKV, 0)],
                5: [(self_scores, SELF, 1), (proj_q, QKV, 1)],
                6: [(self_scores, SELF, 2), (proj_q, QKV, 2)],
                7: [(self_scores, SELF, 3), (proj_q, QKV, 3)],
                9: [(self_shift_T, SELF, 0), (proj_k, QKV, 0)],
                10: [(proj_k, QKV, 1)], 11: [(proj_k, QKV, 2)], 12: [(proj_k, QKV, 3)],
                13: [(self_scores_T, SELF, 0), (proj_v, QKV, 0)],
                14: [(self_scores_T, SELF, 1), (proj_v, QKV, 1)],
                15: [(proj_v, QKV, 2)],
                16: [(self_pv, SELF, 0), (proj_v, QKV, 3)],
                17: [(cross_shift_T, MAX, 0)],
                18: [(self_scores_T, SELF, 2), (quant_T, FFN, 0)],
                19: [(self_scores_T, SELF, 3)],
                20: [(ffn, FFN, 0), (ffn, FFN, 1)],
                21: [(self_pv, SELF, 1), (ffn, FFN, 2)],
                22: [(ffn, FFN, 3)],
                23: [(o_T, SELF, 0)],
                24: [(proj_o, SELF, 0)], 25: [(proj_o, SELF, 1)], 26: [(proj_o, SELF, 2)], 27: [(proj_o, SELF, 3)],
                32: [(cross_shift_T, MAX, 1)],
            }

            def slot(s):
                for n in range(XH * KC + 1):
                    for piece, stage, k in BETWEEN.get(n, ()):
                        if s.has(stage):
                            piece(s, k)
                    if n == XH * KC:
                        break
                    if s.has(CROSS) and n % 2 == 0:
                        cross_scores_T(s, n // 2)
                    if s.has(MAX):
                        cross_scores(s, n)
                    if s.has(CROSS) and n % 4 == 3 and n > 4:
                        cross_pv(s, n // 4 - 1)
                if s.has(CROSS):
                    cross_pv(s, UNITS - 1)

            run(pe, slot)


def kernel(x, ctx_2048, L0_attn_Wqkv, L0_attn_q_norm_w, L0_attn_k_norm_w, L0_attn_Wo, L0_ffn_weight):
    import numpy as np
    import concourse.bacc as bacc
    from concourse.bass_utils import run_bass_kernel_spmd

    S, HD = x.shape[1], x.shape[2] // 16
    inv_freq = (1.0 / 10000.0 ** (np.arange(0, HD, 2, dtype=np.float32) / np.float32(HD))).astype(np.float32)
    freqs = np.arange(S, dtype=np.float32)[:, None] * inv_freq[None, :]
    arrays = {
        "x": x, "ctx": ctx_2048, "wqkv": L0_attn_Wqkv, "q_norm_w": L0_attn_q_norm_w,
        "k_norm_w": L0_attn_k_norm_w, "wo": L0_attn_Wo, "wffn": L0_ffn_weight,
        "rope_cos": np.cos(freqs), "rope_sin": np.sin(freqs),
    }
    arrays = {k: np.ascontiguousarray(v) for k, v in arrays.items()}
    nc = bacc.Bacc("TRN2", target_bir_lowering=False, num_devices=1)
    args = [nc.dram_tensor(k, v.shape, mybir.dt.from_np(v.dtype), kind="ExternalInput").ap()
            for k, v in arrays.items()]
    out = nc.dram_tensor("out", x.shape, mybir.dt.float32, kind="ExternalOutput").ap()
    post_ln_decoder_kernel(nc, *args, out)
    r = run_bass_kernel_spmd(nc, [arrays], core_ids=[0])
    return r.results[0]["out"]
```

```python
import concourse.bass as bass
from concourse import mybir
from contextlib import ExitStack


def post_ln_decoder_kernel(nc, x, ctx_in, wqkv, q_norm_w, k_norm_w, wo, wffn, cos_t, sin_t, out):
    F32, F32R = mybir.dt.float32, mybir.dt.float32r
    BF16, F16, I32 = mybir.dt.bfloat16, mybir.dt.float16, mybir.dt.int32
    ALU, ACT, AX = mybir.AluOpType, mybir.ActivationFunctionType, mybir.AxisListType

    BATCH, TOK, D = x.shape
    P = TOK
    NH, HD = 16, D // 16
    HH = HD // 2
    XH, XD = 8, TOK // 8
    KC = D // P
    HC = NH // KC
    GROUPS, GH = XH // 4, 4
    UNITS = GROUPS * KC
    SELF_SCALE, CROSS_SCALE = HD ** -0.5, XD ** -0.5
    WINDOW = 256
    assert TOK <= WINDOW
    RMS_EPS, LN_EPS = 1e-6, 1e-5
    QBLK, FP8_MAX = 128, 448.0
    NQ = D // QBLK
    SHIFT_UNIT = 64.0
    NEG = -1e30
    SROWS = 3 * HD
    XROWS = 96
    Q_PLANE, K_PLANE = (0, 0, 0, 1, 1), (0, 1, 2, 0, 1)
    N_SC = XH * KC
    EXP_BITS = 0x7F800000
    MIN_NORMAL, MAGIC = 2.0 ** -6, 1.5 * 2.0 ** 20

    qpl_d = nc.dram_tensor("q_planes", [BATCH, 2, TOK, D], F16, kind="Internal").ap()
    kpl_d = nc.dram_tensor("k_planes", [BATCH, 3, TOK, D], BF16, kind="Internal").ap()
    x2_d = nc.dram_tensor("x2_rows", [BATCH, TOK, D], F32, kind="Internal").ap()
    sh1_d = nc.dram_tensor("self_shift", [BATCH, 2 * NH, TOK], F16, kind="Internal").ap()
    sh2_d = nc.dram_tensor("cross_shift", [BATCH, GROUPS, 32, P], F16, kind="Internal").ap()

    es = ExitStack()
    with es:
        def sb(name, shape, dt=F32):
            return es.enter_context(nc.sbuf_tensor(name, shape, dt))

        def bank(name):
            return es.enter_context(nc.psum_tensor(name, [P, 512], F32))

        def sem(name):
            return es.enter_context(nc.semaphore(name))

        w_h, w_l = sb("w_h", [P, KC, 3 * D], F32R), sb("w_l", [P, KC, 3 * D], F32R)
        wo_h, wo_l = sb("wo_h", [P, KC, D], F32R), sb("wo_l", [P, KC, D], F32R)
        wf_h, wf_l = sb("wf_h", [P, KC, D], F32R), sb("wf_l", [P, KC, D], F32R)
        cos_w = [sb(f"cos_w{i}", [P, NH, 2, HH]) for i in range(2)]
        sin_w = [sb(f"sin_w{i}", [P, NH, 2, HH]) for i in range(2)]
        cos_s, sin_s = sb("cos_s", [P, HH]), sb("sin_s", [P, HH])
        ident = sb("ident", [P, P])
        ident16 = sb("ident16", [P, P], F16)
        identb = sb("identb", [P, P], BF16)
        maskb = sb("maskb", [P, P], BF16)
        half = sb("half", [P, 1])
        xb = [sb(f"xb{i}", [P, D]) for i in range(2)]
        cx, cx_rest = sb("cx", [P, D]), sb("cx_rest", [P, D])
        lin_h, lin_l = sb("lin_h", [P, D], F32R), sb("lin_l", [P, D], F32R)
        ropeA, ropeB = sb("ropeA", [P, NH, 2, HH]), sb("ropeB", [P, NH, 2, HH])
        junk = sb("junk", [P, D], BF16)
        qkn = [sb(f"qkn{i}", [P, NH, 3, HD], F16) for i in range(2)]
        va = [sb(f"va{i}", [P, NH, HD + 1]) for i in range(2)]
        qs = sb("qs", [SROWS + 2, NH, P], F16)
        ks = sb("ks", [SROWS + 2, NH, P], F16)
        p1 = [sb(f"p1_{i}", [P, HC, P]) for i in range(2)]
        o1 = sb("o1", [P, D])
        x2 = sb("x2", [P, D])
        qpl = sb("qpl", [P, 2, D], F16)
        kpl = sb("kpl", [P, 3, D], BF16)
        qst = [sb(f"qst{i}", [XROWS + 2, XH, D], F16) for i in range(2)]
        kst = [sb(f"kst{i}", [XROWS + 2, XH, D], BF16) for i in range(2)]
        vT = [sb(f"vT{i}", [P, KC, XH, 2 * XD]) for i in range(2)]
        pp = sb("pp", [P, 2, GH, D])
        o2 = sb("o2", [P, GROUPS, D])
        x3 = sb("x3", [P, D])
        yq, yc = sb("yq", [P, D]), sb("yc", [P, D])
        o2n = yq[:].rearrange("p (c h d) -> p c h d", c=KC, h=XH)
        yout = sb("yout", [P, D])
        ssq, rms = sb("ssq", [P, 2]), sb("rms", [P, 2])
        nm1, sh1 = sb("nm1", [P, NH]), sb("sh1", [P, 2, NH], F16)
        sh1T = sb("sh1T", [2 * NH, P], F16)
        nm2, sh2 = sb("nm2", [P, GROUPS, 16]), sb("sh2", [P, GROUPS, 2, 16], F16)
        sh2T = [sb(f"sh2T{g}", [32, P], F16) for g in range(GROUPS)]
        r1 = sb("r1", [P, 2, NH // 2])
        st6 = [sb(f"st6_{i}", [P, 6]) for i in range(3)]
        mv = [sb(f"mv{i}", [P, 2]) for i in range(3)]
        rstd = [sb(f"rstd{i}", [P, 1]) for i in range(3)]
        r2 = sb("r2", [P, GROUPS, KC, GH])
        amax, qsc, qri = sb("amax", [P, NQ]), sb("qsc", [P, NQ]), sb("qri", [P, NQ])

        st = [bank(f"st{i}") for i in range(2)]
        pv = bank("pv")
        mx = [bank(f"mx{i}") for i in range(2)]
        banks = [bank(f"bank{i}") for i in range(3)]

        d_setup = [sem(f"d_setup{i}") for i in range(2)]
        d_const = sem("d_const")
        d_x = [sem(f"d_x{i}") for i in range(2)]
        d_cx, d_kpl_stored = sem("d_cx"), sem("d_kpl_stored")
        d_x2_stored, d_x3, d_qpl_stored = sem("d_x2_stored"), sem("d_x3"), sem("d_qpl_stored")
        d_qst = [[sem(f"d_qst{i}{g}") for g in range(GROUPS)] for i in range(2)]
        d_kst = [[sem(f"d_kst{i}{g}") for g in range(GROUPS)] for i in range(2)]
        d_sh1_stored, d_sh1 = sem("d_sh1_stored"), sem("d_sh1")
        d_sh2_stored = [sem(f"d_sh2_stored{g}") for g in range(GROUPS)]
        d_sh2 = [sem(f"d_sh2_{g}") for g in range(GROUPS)]
        d_out = sem("d_out")
        u_zero, u_const, u_dve = sem("u_zero"), sem("u_const"), sem("u_dve")
        u_staged, u_fT, u_done = sem("u_staged_used"), sem("u_ffn_transposed"), sem("u_done")
        bank_full = [sem(f"bank_full{i}") for i in range(3)]
        bank_free = [sem(f"bank_free{i}") for i in range(3)]
        mx_full, mx_free = sem("mx_full"), sem("mx_free")
        st_full, st_free = sem("st_full"), sem("st_free")
        pv_unit, pv_free = sem("pv_unit_done"), sem("pv_free")
        passed_sp, passed_pool, passed_dve = sem("passed_sp"), sem("passed_pool"), sem("passed_dve")
        s_xTh, s_oTh, s_xdh = sem("s_xT_high"), sem("s_oT_high"), sem("s_xdT_high")
        s_ssq, s_ms, s_rms = sem("s_ssq"), sem("s_mean_square"), sem("s_rms")
        s_rope, s_part_h, s_part_l = sem("s_rope"), sem("s_part_high"), sem("s_part_low")
        s_sc1, s_h1, s_sh1 = sem("s_shift1_scaled"), sem("s_shift1_high"), sem("s_shift1")
        s_sc2, s_h2, s_sh2 = sem("s_shift2_scaled"), sem("s_shift2_high"), sem("s_shift2")
        s_masked, s_r1, s_r2 = sem("s_masked"), sem("s_r1"), sem("s_r2")
        s_st6, s_mv, s_ve, s_rstd, s_ln = ([sem(f"s_{n}{i}") for i in range(3)]
                                           for n in ("st6_", "mv", "ve", "rstd", "ln"))
        s_qh, s_ql = sem("s_q_high"), sem("s_q_low")
        s_k1, s_kr, s_k2, s_k3 = sem("s_k1"), sem("s_k_rest"), sem("s_k2"), sem("s_k3")
        s_am, s_qsc, s_qri = sem("s_amax"), sem("s_qscale"), sem("s_qrecip")
        s_unit, s_exp, s_magic, s_sum, s_round, s_back = (
            sem(f"s_quant_{n}") for n in ("unit", "exp", "magic", "sum", "round", "back"))

        def steps(text):
            out = []
            for word in text.split():
                name, rest = word.split(":")
                k, stage = rest.split("@")
                out.append((name, int(k), int(stage)))
            return out

        SP_STEPS = steps("""
            ld_sh2:0@3 st_sh1:0@1 ld_kst:0@2 ld_sh1:0@1 ld_cx:0@1 ld_kst:1@2 st_x2:0@2 ld_qst:0@2
            ld_qst:1@2 ld_x:0@0 st_kpl:0@1 st_out:0@4 ld_x2r:0@3 st_sh2:1@3 ld_sh2:1@3 st_qpl:0@1
            st_sh2:0@2""")
        POOL_STEPS = steps("""
            part_low:1@1 layer_rstd:1@4 quant_unit:0@4 mask:0@1 mask:1@1 quant_round:0@4
            quant_round:1@4 mask:2@1 quant_round:2@4 mask:3@1 context_rest:0@1 context_rest:1@1
            layer_rstd:2@4 layer_rstd:0@1 mean_square:0@0 rope_sum:0@0 mean_square:1@0 part_low:0@0
            query_low:0@1 rope_sum:1@0""")
        ACT_STEPS = steps("""
            probs:27@4 probs:28@4 probs:29@4 probs:30@4 probs:31@4 group_out:1@4 self_shift_out:0@1
            probs:0@3 probs:1@3 probs:2@3 probs:3@3 probs:4@3 context_out:0@2 probs:5@3 probs:6@3
            probs:7@3 probs:8@3 probs:9@3 self_probs:0@1 self_probs:1@1 probs:10@3 context_high:0@1
            probs:11@3 self_probs:2@1 probs:12@3 probs:13@3 self_probs:3@1 probs:14@3 xdT_high:0@4
            context_high:1@1 probs:15@3 oT_high:0@1 xT_high:0@0 cross_shift_out:1@3 group_out:0@3
            square:0@0 query_high:0@1 probs:16@3 square:1@0 part_high:0@0 probs:17@3 probs:18@3
            probs:19@3 probs:20@3 self_stack:0@0 probs:21@3 value:0@0 part_high:1@0 probs:22@3
            probs:23@3 probs:24@3 self_stack:1@0 self_stack:2@0 probs:25@3 cross_shift_out:0@2
            self_stack:3@0 probs:26@3""")
        DVE_STEPS = steps("""
            self_max:1@1 self_max:2@1 cross_max:17@3 cross_max:18@3 self_max:3@1 self_shift:0@1
            cross_norm:0@4 cross_norm:1@4 add_cross:0@4 cross_max:19@3 layernorm:1@4 quant_scale:0@4
            cross_max:20@3 cross_max:21@3 quant_magic:0@4 cross_max:22@3 cross_max:23@3 cross_max:24@3
            cross_max:25@3 cross_max:26@3 self_norm:0@1 xdT_low:0@4 cross_max:27@3 cross_max:28@3
            self_norm:1@1 cross_max:29@3 oT_low:0@1 add_ffn:0@4 cross_max:30@3 cross_max:31@3
            layernorm:2@4 cross_shift:1@3 xT_low:0@0 cross_max:0@2 add_self:0@1 cross_max:1@2
            layernorm:0@1 cross_max:2@2 rope_terms:0@0 cross_max:3@2 cross_max:4@2 cross_max:5@2
            cross_max:6@2 cross_max:7@2 rope_terms:1@0 cross_max:8@2 cross_max:9@2 cross_max:10@2
            cross_max:11@2 cross_max:12@2 cross_max:13@2 cross_max:14@2 cross_max:15@2 cross_shift:0@2
            self_max:0@0 cross_max:16@2""")
        PE_STEPS = steps("""
            self_scores:2@1 cross_scores_T:28@4 cross_scores:17@3 cross_scores_T:29@4 cross_pv:6@4
            cross_scores_T:30@4 cross_scores_T:31@4 cross_scores:18@3 self_scores:3@1 group_T:0@4
            cross_pv:7@4 cross_scores_T:0@3 cross_scores:19@3 self_shift_T:0@1 cross_scores_T:1@3
            group_T:1@4 cross_scores_T:2@3 back_T:0@4 cross_scores:20@3 cross_scores_T:3@3
            cross_scores_T:4@3 context_T:0@2 cross_scores_T:5@3 cross_pv:0@3 cross_scores_T:6@3
            cross_scores_T:7@3 cross_scores:21@3 cross_scores_T:8@3 cross_scores_T:9@3
            self_scores_T:0@1 self_scores_T:1@1 cross_pv:1@3 cross_scores_T:10@3 cross_scores_T:11@3
            cross_scores:22@3 self_scores_T:2@1 self_pv:0@1 cross_scores:23@3 cross_scores_T:12@3
            cross_scores_T:13@3 self_scores_T:3@1 cross_scores:24@3 cross_scores_T:14@3
            cross_scores:25@3 cross_scores:26@3 cross_scores_T:15@3 quant_T:0@4 cross_scores:27@3
            cross_scores:28@3 self_pv:1@1 ffn:0@4 cross_scores:29@3 ffn:1@4 ffn:2@4 ffn:3@4 o_T:0@1
            cross_pv:2@3 cross_scores:30@3 cross_scores:31@3 proj_o:0@1 proj_o:1@1 proj_o:2@1
            proj_o:3@1 x_T:0@0 cross_pv:3@3 cross_shift_T:1@3 cross_scores:0@2 cross_scores:1@2
            proj_q:0@0 proj_q:1@0 proj_q:2@0 proj_q:3@0 proj_k:0@0 cross_scores:2@2 proj_k:1@0
            cross_scores:3@2 proj_k:2@0 proj_k:3@0 cross_scores_T:16@3 proj_v:0@0 cross_scores:4@2
            cross_scores_T:17@3 cross_scores:5@2 proj_v:1@0 cross_scores_T:18@3 cross_scores:6@2
            cross_scores:7@2 proj_v:2@0 cross_scores_T:19@3 cross_scores:8@2 cross_scores_T:20@3
            parts_T:0@0 cross_scores_T:21@3 proj_v:3@0 cross_scores:9@2 cross_pv:4@3 cross_scores:10@2
            parts_T:1@0 cross_scores:11@2 cross_scores_T:22@3 cross_scores:12@2 cross_scores_T:23@3
            cross_scores:13@2 cross_scores_T:24@3 cross_scores:14@2 cross_scores_T:25@3 parts_T:2@0
            cross_scores:15@2 cross_pv:5@3 parts_T:3@0 cross_shift_T:0@2 self_scores:0@0
            cross_scores_T:26@3 cross_scores:16@2 cross_scores_T:27@3 self_scores:1@0""")

        BANK = {
            "xT": 0, "q": 0, "k": 1, "v": 2, "tqk0": 0, "tqk1": 0, "tqk2": 2, "tqk3": 1, "s1m0": 2,
            "s1m1": 0, "s1m2": 1, "s1m3": 2, "m1T": 0, "s1t0": 2, "s1t1": 0, "s1t2": 1, "s1t3": 2,
            "pv10": 0, "pv11": 1, "oT": 1, "wo": 1, "vT": 2, "mT0": 0, "mT1": 2, "o2T0": 1, "o2T1": 2,
            "o2N": 1, "xdT": 2, "ffn": 0}
        OPENS = {("x_T", 0): "xT", ("proj_q", 0): "q", ("proj_k", 0): "k", ("proj_v", 0): "v",
                 ("self_shift_T", 0): "m1T", ("o_T", 0): "oT", ("proj_o", 0): "wo", ("context_T", 0): "vT",
                 ("back_T", 0): "o2N", ("quant_T", 0): "xdT", ("ffn", 0): "ffn"}
        OPENS.update({(name, k): f"{turn}{k}" for name, turn, n in (
            ("parts_T", "tqk", 4), ("self_scores", "s1m", KC), ("self_scores_T", "s1t", KC),
            ("self_pv", "pv1", 2), ("cross_shift_T", "mT", GROUPS), ("group_T", "o2T", GROUPS))
            for k in range(n)})
        TURNS = [[(OPENS[name, k], stage) for name, k, stage in PE_STEPS
                  if (name, k) in OPENS and BANK[OPENS[name, k]] == i] for i in range(3)]

        LAST = max(stage for table in (SP_STEPS, POOL_STEPS, ACT_STEPS, DVE_STEPS, PE_STEPS)
                   for _, _, stage in table)
        SLOTS = BATCH + LAST
        LOOP0 = LAST + 3
        ROUNDS = (BATCH - LOOP0) // 2 - 1

        class Count:

            def __init__(self, b, rnd):
                self.b, self.rnd, self.i = b, rnd, b % 2

            def idx(self):
                return self.b if self.rnd is None else self.rnd * 2 + self.b

            def n(self, per, k):
                v = self.b * per + k
                return max(v, 0) if self.rnd is None else self.rnd * (2 * per) + v

            def n2(self, per, k):
                v = (self.b // 2) * per + k
                return v if self.rnd is None else self.rnd * per + v

        def turns_done(name, b, ahead=0, own=1):
            turns = TURNS[BANK[name]]
            at = [n for n, _ in turns].index(name)
            batch = b.b + ahead
            if batch < 0:
                return 0
            t = batch + turns[at][1]
            v = own + sum(0 <= t0 - stage < BATCH for t0 in range(t) for _, stage in turns)
            v += sum(0 <= t - stage < BATCH for _, stage in turns[:at])
            if b.rnd is None:
                return v
            assert t >= LAST and t + 2 * ROUNDS <= BATCH
            return b.rnd * (2 * len(turns)) + v

        def full(name, b, ahead=0):
            return bank_full[BANK[name]], turns_done(name, b, ahead)

        def freed(name, b, ahead=0):
            return bank_free[BANK[name]], turns_done(name, b, ahead)

        def before(name, b):
            return bank_free[BANK[name]], turns_done(name, b, 0, 0)

        def run(eng, table, fns):
            def slot(t, rnd=None):
                for name, k, stage in table:
                    if 0 <= t - stage < BATCH:
                        fns[name](Count(t - stage, rnd), k)

            for t in range(LOOP0):
                slot(t)
            with eng.Fori(0, ROUNDS) as rnd:
                for u in range(2):
                    slot(LOOP0 + u, rnd)
            for t in range(LOOP0 + 2 * ROUNDS, SLOTS):
                slot(t)

        def at(name):
            return banks[BANK[name]]

        U_CONST = 4 + 1 + 5 * 2 + 1

        block = es.enter_context(nc.Block())

        @block.sync
        def _(sp):
            sp.dma_start(cos_s[:], cos_t).then_inc(d_const, 16)
            sp.dma_start(sin_s[:], sin_t).then_inc(d_const, 16)
            for dst, w in ((ropeA, q_norm_w), (ropeB, k_norm_w)):
                sp.dma_start(dst[:].rearrange("p h a d -> p (h a d)"), w.partition_broadcast(P)).then_inc(d_const, 16)
            for n in range(3 * KC):
                if n >= 2:
                    sp.wait_ge(u_staged, n - 1)
                src = (wqkv, wo, wffn)[n // KC][(n % KC) * P:(n % KC + 1) * P, :]
                sp.dma_start(pp[:, n % 2].rearrange("p a d -> p (a d)")[:, 0:src.shape[1]], src)\
                  .then_inc(d_setup[n % 2], 16)
            sp.wait_ge(u_const, U_CONST)

            def ld_x(b, _):
                sp.wait_ge(*freed("wo", b, -2))
                sp.sem_inc(passed_sp, 1)
                sp.dma_start(xb[b.i][:], x[b.idx()]).then_inc(d_x[b.i], 16)

            def ld_cx(b, _):
                sp.wait_ge(s_kr, b.n(1, 0))
                sp.sem_inc(passed_sp, 1)
                sp.wait_ge(*full("vT", b, -1))
                sp.sem_inc(passed_sp, 1)
                sp.dma_start(cx[:], ctx_in[b.idx()]).then_inc(d_cx, 16)

            def st_kpl(b, _):
                sp.wait_ge(s_k3, b.n(1, 1))
                sp.sem_inc(passed_sp, 1)
                sp.dma_start(kpl_d[b.idx()].rearrange("g p n -> p g n"), kpl[:]).then_inc(d_kpl_stored, 16)

            def ld_kst(b, g):
                sp.wait_ge(d_kpl_stored, b.n(16, 16))
                sp.sem_inc(passed_sp, 1)
                sp.wait_ge(st_full, b.n(N_SC, N_SC // GROUPS * (g + 1) - 2 * N_SC))
                sp.sem_inc(passed_sp, 1)
                for r in range(5):
                    sp.dma_start(kst[b.i][r * XD:(r + 1) * XD, GH * g:GH * (g + 1), :],
                                 kpl_d[b.idx()][K_PLANE[r]][GH * g * XD:GH * (g + 1) * XD, :]
                                 .rearrange("(h d) n -> d h n", d=XD)).then_inc(d_kst[b.i][g], 16)

            def ld_qst(b, g):
                sp.wait_ge(d_qpl_stored, b.n(16, 16))
                sp.sem_inc(passed_sp, 1)
                sp.wait_ge(st_full, b.n(N_SC, N_SC // GROUPS * (g + 1) - 2 * N_SC))
                sp.sem_inc(passed_sp, 1)
                for r in range(5):
                    sp.dma_start(qst[b.i][r * XD:(r + 1) * XD, GH * g:GH * (g + 1), :],
                                 qpl_d[b.idx()][Q_PLANE[r]][GH * g * XD:GH * (g + 1) * XD, :]
                                 .rearrange("(h d) n -> d h n", d=XD)).then_inc(d_qst[b.i][g], 16)

            def st_sh1(b, _):
                sp.wait_ge(*freed("m1T", b))
                sp.sem_inc(passed_sp, 1)
                sp.dma_start(sh1_d[b.idx()], sh1T[:]).then_inc(d_sh1_stored, 16)

            def ld_sh1(b, _):
                sp.wait_ge(d_sh1_stored, b.n(16, 16))
                sp.sem_inc(passed_sp, 1)
                sp.wait_ge(*full(f"s1t{KC - 1}", b, -1))
                sp.sem_inc(passed_sp, 1)
                sp.dma_start(qs[SROWS:SROWS + 2, :, :],
                             sh1_d[b.idx()].rearrange("(a h) q -> a h q", a=2)).then_inc(d_sh1, 16)

            def st_sh2(b, g):
                sp.wait_ge(*freed(f"mT{g}", b))
                sp.sem_inc(passed_sp, 1)
                sp.dma_start(sh2_d[b.idx()][g], sh2T[g][:]).then_inc(d_sh2_stored[g], 16)

            def ld_sh2(b, g):
                sp.wait_ge(d_sh2_stored[g], b.n(16, 16))
                sp.sem_inc(passed_sp, 1)
                sp.wait_ge(st_full, b.n(N_SC, N_SC // GROUPS * (g + 1) - 2 * N_SC))
                sp.sem_inc(passed_sp, 1)
                sp.dma_start(qst[b.i][XROWS:XROWS + 2, GH * g:GH * (g + 1), :]
                             .rearrange("a h (c m) -> a (h c) m", c=KC),
                             sh2_d[b.idx()][g].rearrange("(a r) m -> a r m", a=2)).then_inc(d_sh2[g], 16)

            def st_x2(b, _):
                sp.wait_ge(s_ln[0], b.n(1, 1))
                sp.sem_inc(passed_sp, 1)
                sp.dma_start(x2_d[b.idx()], x2[:]).then_inc(d_x2_stored, 16)

            def st_qpl(b, _):
                sp.wait_ge(s_ql, b.n(1, 1))
                sp.sem_inc(passed_sp, 1)
                sp.dma_start(qpl_d[b.idx()].rearrange("g p n -> p g n"), qpl[:]).then_inc(d_qpl_stored, 16)

            def ld_x2r(b, _):
                sp.wait_ge(d_x2_stored, b.n(16, 16))
                sp.sem_inc(passed_sp, 1)
                sp.wait_ge(*freed("ffn", b, -1))
                sp.sem_inc(passed_sp, 1)
                sp.dma_start(x3[:], x2_d[b.idx()]).then_inc(d_x3, 16)

            def st_out(b, _):
                sp.wait_ge(s_ln[2], b.n(1, 1))
                sp.sem_inc(passed_sp, 1)
                sp.dma_start(out[b.idx()], yout[:]).then_inc(d_out, 16)

            run(sp, SP_STEPS, {
                "ld_x": ld_x, "ld_cx": ld_cx, "st_kpl": st_kpl, "ld_kst": ld_kst, "ld_qst": ld_qst,
                "st_sh1": st_sh1, "ld_sh1": ld_sh1, "st_sh2": st_sh2, "ld_sh2": ld_sh2,
                "st_x2": st_x2, "st_qpl": st_qpl, "ld_x2r": ld_x2r, "st_out": st_out})
            sp.wait_ge(d_out, 16 * BATCH)

        @block.gpsimd
        def _(pool):
            g_ = nc.gpsimd
            for m in (ident, ident16, identb, maskb):
                g_.memset(m[:], 0.0).then_inc(u_zero, 1)
            pool.wait_ge(u_zero, 4)
            for m in (ident, ident16, identb):
                g_.affine_select(out=m[:], in_=m[:], compare_op=ALU.not_equal, fill=1.0, base=0,
                                 pattern=[[-1, P]], channel_multiplier=1).then_inc(u_const, 1)
            g_.affine_select(out=maskb[:], in_=maskb[:], compare_op=ALU.is_ge, fill=NEG, base=0,
                             pattern=[[-1, P]], channel_multiplier=1).then_inc(u_const, 1)
            g_.memset(half[:], -0.5).then_inc(u_const, 1)
            n = 5
            for rows, value in [r for i in range(2) for r in (
                    (va[i][:, :, HD:HD + 1], 1.0), (vT[i][:, :, :, XD:2 * XD], 1.0),
                    (qst[i][64:XROWS, :, :], 0.0), (kst[i][64:XROWS, :, :], 0.0),
                    (kst[i][XROWS:XROWS + 2, :, :], SHIFT_UNIT))] + [(ks[SROWS:SROWS + 2, :, :], SHIFT_UNIT)]:
                pool.wait_ge(u_const, n)
                g_.memset(rows, value).then_inc(u_const, 1)
                n += 1
            pool.wait_ge(u_const, U_CONST)
            pool.wait_ge(u_done, 1)

            def mean_square(b, k):
                pool.wait_ge(s_ssq, b.n(2, k + 1))
                pool.sem_inc(passed_pool, 1)
                g_.tensor_scalar(rms[:, k:k + 1], ssq[:, k:k + 1], 1.0 / D, RMS_EPS, ALU.mult, ALU.add)\
                  .then_inc(s_ms, 1)
                pool.wait_ge(s_ms, b.n(2, k + 1))
                g_.tensor_tensor(rms[:, k:k + 1], rms[:, k:k + 1], half[:], ALU.pow).then_inc(s_rms, 1)

            def layer_rstd(b, i):
                pool.wait_ge(s_mv[i], b.n(1, 1))
                pool.sem_inc(passed_pool, 1)
                g_.tensor_scalar(rstd[i][:], mv[i][:, 1:2], 1.0, LN_EPS, ALU.mult, ALU.add).then_inc(s_ve[i], 1)
                pool.wait_ge(s_ve[i], b.n(1, 1))
                g_.tensor_tensor(rstd[i][:], rstd[i][:], half[:], ALU.pow).then_inc(s_rstd[i], 1)

            def rope_sum(b, k):
                pool.wait_ge(*freed("qk"[k], b))
                g_.tensor_tensor(ropeA[:], ropeA[:], ropeB[:], ALU.add).then_inc(s_rope, 1)

            def part_low(b, k):
                pool.wait_ge(s_part_h, b.n(2, k + 1))
                g_.tensor_tensor(qkn[k][:, :, 2 - k, :], ropeA[:].rearrange("p h a d -> p h (a d)"),
                                 qkn[k][:, :, 0, :], ALU.subtract).then_inc(s_part_l, 1)

            def mask(b, c):
                pool.wait_ge(*freed(f"s1t{c}", b))
                pool.sem_inc(passed_pool, 1)
                g_.affine_select(out=p1[c % 2][:], in_=p1[c % 2][:], compare_op=ALU.is_ge, fill=0.0, base=0,
                                 pattern=[[0, HC], [1, P]], channel_multiplier=-1).then_inc(s_masked, 1)

            def context_rest(b, k):
                if k == 0:
                    pool.wait_ge(s_k1, b.n(1, 1))
                    g_.tensor_tensor(cx_rest[:], cx[:], kpl[:, 0, :], ALU.subtract).then_inc(s_kr, 1)
                else:
                    pool.wait_ge(s_k2, b.n(1, 1))
                    g_.tensor_tensor(kpl[:, 2, :], cx_rest[:], kpl[:, 1, :], ALU.subtract).then_inc(s_k3, 1)

            yq_blocks = yq[:].rearrange("p (n k) -> p n k", n=NQ)

            def quant_unit(b, _):
                pool.wait_ge(s_qri, b.n(1, 1))
                g_.tensor_tensor(yq_blocks, x3[:].rearrange("p (n k) -> p n k", n=NQ),
                                 qri[:].unsqueeze(2).to_broadcast([P, NQ, QBLK]), ALU.mult).then_inc(s_unit, 1)

            def quant_round(b, step):
                if step == 0:
                    pool.wait_ge(s_magic, b.n(1, 1))
                    g_.tensor_tensor(yq[:], yq[:], yc[:], ALU.add).then_inc(s_sum, 1)
                elif step == 1:
                    pool.wait_ge(s_sum, b.n(1, 1))
                    g_.tensor_tensor(yq[:], yq[:], yc[:], ALU.subtract).then_inc(s_round, 1)
                else:
                    pool.wait_ge(s_round, b.n(1, 1))
                    g_.tensor_tensor(yq_blocks, yq_blocks, qsc[:].unsqueeze(2).to_broadcast([P, NQ, QBLK]), ALU.mult)\
                      .then_inc(s_back, 1)

            def query_low(b, _):
                pool.wait_ge(s_qh, b.n(1, 1))
                g_.tensor_tensor(qpl[:, 1, :], x2[:], qpl[:, 0, :], ALU.subtract).then_inc(s_ql, 1)

            run(pool, POOL_STEPS, {
                "mean_square": mean_square, "layer_rstd": layer_rstd, "rope_sum": rope_sum,
                "part_low": part_low, "mask": mask, "context_rest": context_rest,
                "quant_unit": quant_unit, "quant_round": quant_round, "query_low": query_low})

        @block.scalar
        def _(act):
            a = nc.scalar
            act.wait_ge(u_done, 1)
            act.wait_ge(u_const, U_CONST)

            def probs(b, n):
                unit, j = n // GH, n % GH
                act.wait_ge(st_full, b.n(N_SC, n + 1))
                act.wait_ge(pv_unit, b.n(UNITS, unit - 1))
                a.activation(pp[:, unit % 2, j, :], st[n % 2][:], ACT.Exp, scale=CROSS_SCALE).then_inc(st_free, 1)

            def group_out(b, g):
                act.wait_ge(pv_unit, b.n(UNITS, KC * (g + 1)))
                act.wait_ge(*full(f"o2T{g}", b, -1))
                a.activation(o2[:, g, :], pv[:], ACT.Copy).then_inc(pv_free, 1)

            def xT_high(b, _):
                act.wait_ge(*full("xT", b))
                a.activation(lin_h[:], at("xT")[:], ACT.Copy).then_inc(s_xTh, 1)

            def square(b, k):
                act.wait_ge(*full("qk"[k], b))
                act.wait_ge(s_ms, b.n(2, k - 1))
                act.wait_ge(s_ssq, b.n(2, k))
                a.activation(junk[:], at("qk"[k])[:], ACT.Square, accum_out=ssq[:, k:k + 1]).then_inc(s_ssq, 1)

            def part_high(b, k):
                act.wait_ge(s_rope, b.n(2, k + 1))
                act.wait_ge(*full(f"tqk{2 * k + 1}", b, -1))
                src = ropeA[:].rearrange("p h a d -> p h (a d)")
                a.activation(qkn[k][:, :, 0, :], src, ACT.Copy)
                a.activation(qkn[k][:, :, 1 + k, :], src, ACT.Copy).then_inc(s_part_h, 1)

            def value(b, _):
                act.wait_ge(*full("v", b))
                act.wait_ge(*full("pv11", b, -2))
                a.activation(va[b.i][:, :, 0:HD], at("v")[:].rearrange("p (h d) -> p h d", h=NH), ACT.Copy)\
                 .then_inc(bank_free[BANK["v"]], 1)

            def self_stack(b, i):
                act.wait_ge(*full(f"tqk{i}", b))
                act.wait_ge(*full(f"s1t{2 * (i % 2) + 1}", b, -1))
                dst = (qs, ks)[i // 2][0:SROWS, 8 * (i % 2):8 * (i % 2) + 8, :]
                a.activation(dst, at(f"tqk{i}")[0:SROWS, :].bitcast(F16).rearrange("p (h t) -> p h t", h=8), ACT.Copy)\
                 .then_inc(bank_free[BANK[f"tqk{i}"]], 1)

            def self_shift_out(b, _):
                act.wait_ge(*full("m1T", b))
                act.wait_ge(d_sh1_stored, b.n(16, 0))
                a.activation(sh1T[:], at("m1T")[0:2 * NH, 0:P // 2].bitcast(F16), ACT.Copy)\
                 .then_inc(bank_free[BANK["m1T"]], 1)

            def self_probs(b, c):
                act.wait_ge(*full(f"s1t{c}", b))
                act.wait_ge(*(full("pv11", b, -1) if c < 2 else full("pv10", b)))
                a.activation(p1[c % 2][:], at(f"s1t{c}")[:].rearrange("p (h q) -> p h q", h=HC), ACT.Exp,
                             scale=SELF_SCALE).then_inc(bank_free[BANK[f"s1t{c}"]], 1)

            def oT_high(b, _):
                act.wait_ge(*full("oT", b))
                a.activation(lin_h[:], at("oT")[:], ACT.Copy).then_inc(s_oTh, 1)

            def query_high(b, _):
                act.wait_ge(s_ln[0], b.n(1, 1))
                act.wait_ge(d_qpl_stored, b.n(16, 0))
                a.activation(qpl[:, 0, :], x2[:], ACT.Copy).then_inc(s_qh, 1)

            def context_high(b, k):
                if k == 0:
                    act.wait_ge(d_cx, b.n(16, 16))
                    act.wait_ge(d_kpl_stored, b.n(16, 0))
                    a.activation(kpl[:, 0, :], cx[:], ACT.Copy).then_inc(s_k1, 1)
                else:
                    act.wait_ge(s_kr, b.n(1, 1))
                    a.activation(kpl[:, 1, :], cx_rest[:], ACT.Copy).then_inc(s_k2, 1)

            def context_out(b, _):
                act.wait_ge(*full("vT", b))
                act.wait_ge(pv_unit, b.n(UNITS, -UNITS))
                a.activation(vT[b.i][:, :, :, 0:XD], at("vT")[:].rearrange("p (i h d) -> p i h d", i=KC, h=XH),
                             ACT.Copy).then_inc(bank_free[BANK["vT"]], 1)

            def cross_shift_out(b, g):
                act.wait_ge(*full(f"mT{g}", b))
                act.wait_ge(d_sh2_stored[g], b.n(16, 0))
                a.activation(sh2T[g][:], at(f"mT{g}")[0:32, 0:P // 2].bitcast(F16), ACT.Copy)\
                 .then_inc(bank_free[BANK[f"mT{g}"]], 1)

            def xdT_high(b, _):
                act.wait_ge(*full("xdT", b))
                a.activation(lin_h[:], at("xdT")[:], ACT.Copy).then_inc(s_xdh, 1)

            run(act, ACT_STEPS, {
                "probs": probs, "group_out": group_out, "xT_high": xT_high, "square": square,
                "part_high": part_high, "value": value, "self_stack": self_stack,
                "self_shift_out": self_shift_out, "self_probs": self_probs, "oT_high": oT_high,
                "query_high": query_high, "context_high": context_high, "context_out": context_out,
                "cross_shift_out": cross_shift_out, "xdT_high": xdT_high})

        @block.vector
        def _(dve):
            v = nc.vector
            done = [0]

            def step(ins):
                done[0] += 1
                ins.then_inc(u_dve, 1)
                dve.wait_ge(u_dve, done[0])

            dve.wait_ge(d_const, 64)
            for i, w in enumerate((ropeA, ropeB)):
                v.tensor_tensor(cos_w[i][:], w[:], cos_s[:].unsqueeze(1).unsqueeze(1).to_broadcast([P, NH, 2, HH]),
                                ALU.mult)
                sin_b = sin_s[:].unsqueeze(1).to_broadcast([P, NH, HH])
                v.scalar_tensor_tensor(sin_w[i][:, :, 0, :], w[:, :, 1, :], -1.0, sin_b, ALU.mult, ALU.mult)
                step(v.tensor_tensor(sin_w[i][:, :, 1, :], w[:, :, 0, :], sin_b, ALU.mult))
            for n in range(3 * KC):
                c, piece = n % KC, pp[:, n % 2].rearrange("p a d -> p (a d)")
                dve.wait_ge(d_setup[n % 2], 16 * (n // 2 + 1))
                if n < 2 * KC:
                    hi, lo = ((w_h, w_l), (wo_h, wo_l))[n // KC]
                    src = piece[:, 0:hi.shape[2]]
                    step(v.tensor_copy(hi[:, c, :], src))
                    v.tensor_tensor(lo[:, c, :], src, hi[:, c, :].bitcast(F32), ALU.subtract).then_inc(u_staged, 1)
                    continue
                src = piece[:, 0:D].rearrange("p (n k) -> p n k", n=NQ)
                y3 = yq[:].rearrange("p (n k) -> p n k", n=NQ)
                if c:
                    dve.wait_ge(u_fT, c)
                step(v.tensor_reduce(amax[:], src, AX.X, ALU.max, apply_absolute_value=True))
                step(v.tensor_scalar(qsc[:], amax[:], 1.0 / FP8_MAX, None, ALU.mult))
                step(v.reciprocal(qri[:], qsc[:]))
                step(v.tensor_tensor(y3, src, qri[:].unsqueeze(2).to_broadcast([P, NQ, QBLK]), ALU.mult))
                step(v.tensor_scalar(yc[:].bitcast(I32), yq[:].bitcast(I32), EXP_BITS, None, ALU.bitwise_and))
                step(v.tensor_scalar(yc[:], yc[:], MIN_NORMAL, MAGIC, ALU.max, ALU.mult))
                step(v.tensor_tensor(yq[:], yq[:], yc[:], ALU.add))
                step(v.tensor_tensor(yq[:], yq[:], yc[:], ALU.subtract))
                v.tensor_tensor(y3, y3, qsc[:].unsqueeze(2).to_broadcast([P, NQ, QBLK]), ALU.mult)\
                 .then_inc(u_staged, 1)
                dve.wait_ge(u_fT, c + 1)
                t4 = mx[0][:].rearrange("p (k o) -> p k o", k=KC)
                cols = slice(c * P, (c + 1) * P)
                step(v.tensor_copy(wf_h[:, :, cols], t4))
                step(v.tensor_tensor(wf_l[:, :, cols], t4, wf_h[:, :, cols].bitcast(F32), ALU.subtract))
            v.memset(r1[:], 0.0).then_inc(u_done, 1)
            dve.wait_ge(u_done, 1)

            def cross_max(b, n):
                dve.wait_ge(mx_full, b.n(N_SC, n + 1))
                v.tensor_reduce(nm2[:, n // 16, n % 16:n % 16 + 1], mx[n % 2][:], AX.X, ALU.max, negate=True)\
                 .then_inc(mx_free, 1)

            def cross_shift(b, g):
                dve.wait_ge(mx_free, b.n(N_SC, 16 * (g + 1)))
                v.tensor_scalar(nm2[:, g, :], nm2[:, g, :], 1.0 / SHIFT_UNIT, None, ALU.mult).then_inc(s_sc2, 1)
                dve.wait_ge(s_sc2, b.n(GROUPS, g + 1))
                v.tensor_copy(sh2[:, g, 0, :], nm2[:, g, :]).then_inc(s_h2, 1)
                dve.wait_ge(s_h2, b.n(GROUPS, g + 1))
                v.tensor_tensor(sh2[:, g, 1, :], nm2[:, g, :], sh2[:, g, 0, :], ALU.subtract).then_inc(s_sh2, 1)

            def self_max(b, c):
                dve.wait_ge(*full(f"s1m{c}", b))
                v.tensor_reduce(nm1[:, HC * c:HC * (c + 1)], at(f"s1m{c}")[:].rearrange("p (h k) -> p h k", h=HC),
                                AX.X, ALU.max, negate=True).then_inc(bank_free[BANK[f"s1m{c}"]], 1)

            def self_shift(b, _):
                dve.wait_ge(*freed(f"s1m{KC - 1}", b))
                for c in range(KC - 1):
                    dve.wait_ge(*freed(f"s1m{c}", b))
                v.tensor_scalar(nm1[:], nm1[:], 1.0 / SHIFT_UNIT, None, ALU.mult).then_inc(s_sc1, 1)
                dve.wait_ge(s_sc1, b.n(1, 1))
                v.tensor_copy(sh1[:, 0, :], nm1[:]).then_inc(s_h1, 1)
                dve.wait_ge(s_h1, b.n(1, 1))
                v.tensor_tensor(sh1[:, 1, :], nm1[:], sh1[:, 0, :], ALU.subtract).then_inc(s_sh1, 1)

            def xT_low(b, _):
                dve.wait_ge(s_xTh, b.n(1, 1))
                v.tensor_tensor(lin_l[:], at("xT")[:], lin_h[:].bitcast(F32), ALU.subtract)\
                 .then_inc(bank_free[BANK["xT"]], 1)

            def rope_terms(b, k):
                dve.wait_ge(s_rms, b.n(2, k + 1))
                dve.wait_ge(s_part_l, b.n(2, k))
                rows = at("qk"[k])
                src = rows[:].rearrange("p (h a d) -> p h a d", h=NH, a=2)
                v.scalar_tensor_tensor(ropeA[:].rearrange("p h a d -> p (h a d)"), rows[:], rms[:, k:k + 1],
                                       cos_w[k][:].rearrange("p h a d -> p (h a d)"), ALU.mult, ALU.mult)
                v.scalar_tensor_tensor(ropeB[:, :, 0, :], src[:, :, 1, :], rms[:, k:k + 1], sin_w[k][:, :, 0, :],
                                       ALU.mult, ALU.mult)
                v.scalar_tensor_tensor(ropeB[:, :, 1, :], src[:, :, 0, :], rms[:, k:k + 1], sin_w[k][:, :, 1, :],
                                       ALU.mult, ALU.mult).then_inc(bank_free[BANK["qk"[k]]], 1)

            def self_norm(b, i):
                dve.wait_ge(*full(f"pv1{i}", b))
                src = at(f"pv1{i}")[:, 0:8 * (HD + 1)].rearrange("p (h d) -> p h d", h=8)
                v.reciprocal(r1[:, i, :].unsqueeze(2), src[:, :, HD:HD + 1]).then_inc(s_r1, 1)
                dve.wait_ge(s_r1, b.n(2, i + 1))
                dve.wait_ge(*full("oT", b, -1))
                v.tensor_tensor(o1[:, 8 * HD * i:8 * HD * (i + 1)].rearrange("p (h d) -> p h d", h=8),
                                src[:, :, 0:HD], r1[:, i, :].unsqueeze(2).to_broadcast([P, 8, HD]), ALU.mult)\
                 .then_inc(bank_free[BANK[f"pv1{i}"]], 1)

            def oT_low(b, _):
                dve.wait_ge(s_oTh, b.n(1, 1))
                v.tensor_tensor(lin_l[:], at("oT")[:], lin_h[:].bitcast(F32), ALU.subtract)\
                 .then_inc(bank_free[BANK["oT"]], 1)

            def layernorm_stats(b, i, rows):
                v.bn_stats(st6[i][:], rows[:]).then_inc(s_st6[i], 1)
                dve.wait_ge(s_st6[i], b.n(1, 1))
                dve.sem_inc(passed_dve, 1)
                v.bn_aggr(mv[i][:], st6[i][:]).then_inc(s_mv[i], 1)

            def layernorm(b, i):
                rows = (x2, x3, yout)[i]
                dve.wait_ge(s_rstd[i], b.n(1, 1))
                v.tensor_scalar(rows[:], rows[:], mv[i][:, 0:1], rstd[i][:], ALU.subtract, ALU.mult)\
                 .then_inc(s_ln[i], 1)

            def add_self(b, _):
                dve.wait_ge(*full("wo", b))
                dve.wait_ge(d_x2_stored, b.n(16, 0))
                dve.wait_ge(s_ql, b.n(1, 0))
                v.tensor_tensor(x2[:], at("wo")[:], xb[b.i][:], ALU.add).then_inc(bank_free[BANK["wo"]], 1)
                dve.wait_ge(*freed("wo", b))
                layernorm_stats(b, 0, x2)

            def cross_norm(b, g):
                dve.wait_ge(*full(f"o2T{g}", b))
                src = at(f"o2T{g}")[:].rearrange("p (c j d) -> p c j d", c=KC, j=GH)
                v.reciprocal(r2[:, g].unsqueeze(3), src[:, :, :, XD:XD + 1]).then_inc(s_r2, 1)
                dve.wait_ge(s_r2, b.n(GROUPS, g + 1))
                dve.wait_ge(*full("xdT", b, -1))
                v.tensor_tensor(o2n[:, :, GH * g:GH * (g + 1), :], src[:, :, :, 0:XD],
                                r2[:, g].unsqueeze(3).to_broadcast([P, KC, GH, XD]), ALU.mult)\
                 .then_inc(bank_free[BANK[f"o2T{g}"]], 1)

            def add_cross(b, _):
                dve.wait_ge(*full("o2N", b))
                dve.wait_ge(d_x3, b.n(16, 16))
                v.tensor_tensor(x3[:], at("o2N")[:], x3[:], ALU.add).then_inc(bank_free[BANK["o2N"]], 1)
                dve.wait_ge(*freed("o2N", b))
                layernorm_stats(b, 1, x3)

            def quant_scale(b, _):
                dve.wait_ge(s_ln[1], b.n(1, 1))
                v.tensor_reduce(amax[:], x3[:].rearrange("p (n k) -> p n k", n=NQ), AX.X, ALU.max,
                                apply_absolute_value=True).then_inc(s_am, 1)
                dve.wait_ge(s_am, b.n(1, 1))
                v.tensor_scalar(qsc[:], amax[:], 1.0 / FP8_MAX, None, ALU.mult).then_inc(s_qsc, 1)
                dve.wait_ge(s_qsc, b.n(1, 1))
                v.reciprocal(qri[:], qsc[:]).then_inc(s_qri, 1)

            def quant_magic(b, _):
                dve.wait_ge(s_unit, b.n(1, 1))
                v.tensor_scalar(yc[:].bitcast(I32), yq[:].bitcast(I32), EXP_BITS, None, ALU.bitwise_and)\
                 .then_inc(s_exp, 1)
                dve.wait_ge(s_exp, b.n(1, 1))
                v.tensor_scalar(yc[:], yc[:], MIN_NORMAL, MAGIC, ALU.max, ALU.mult).then_inc(s_magic, 1)

            def xdT_low(b, _):
                dve.wait_ge(s_xdh, b.n(1, 1))
                v.tensor_tensor(lin_l[:], at("xdT")[:], lin_h[:].bitcast(F32), ALU.subtract)\
                 .then_inc(bank_free[BANK["xdT"]], 1)

            def add_ffn(b, _):
                dve.wait_ge(*full("ffn", b))
                dve.wait_ge(d_out, b.n(16, 0))
                v.tensor_tensor(yout[:], at("ffn")[:], x3[:], ALU.add).then_inc(bank_free[BANK["ffn"]], 1)
                dve.wait_ge(*freed("ffn", b))
                layernorm_stats(b, 2, yout)

            run(dve, DVE_STEPS, {
                "cross_max": cross_max, "cross_shift": cross_shift, "self_max": self_max,
                "self_shift": self_shift, "xT_low": xT_low, "rope_terms": rope_terms,
                "self_norm": self_norm, "oT_low": oT_low, "layernorm": layernorm, "add_self": add_self,
                "cross_norm": cross_norm, "add_cross": add_cross, "quant_scale": quant_scale,
                "quant_magic": quant_magic, "xdT_low": xdT_low, "add_ffn": add_ffn})

        @block.tensor
        def _(pe):
            t = nc.tensor
            pe.wait_ge(u_const, U_CONST)
            for c in range(KC):
                pe.wait_ge(u_staged, 2 * KC + c + 1)
                for k in range(KC):
                    last = t.transpose(mx[0][:, k * P:(k + 1) * P], yq[:, k * P:(k + 1) * P], ident[:])
                last.then_inc(u_fT, 1)
            pe.wait_ge(u_done, 1)

            def blocks(dst, src, idm=ident):
                for c in range(KC):
                    last = t.transpose(dst[:, c * P:(c + 1) * P], src(c), idm[:])
                return last

            def linear(name, wh, wl, cols, part):
                rows = slice(part * P, (part + 1) * P)
                for i, (a, w) in enumerate(((lin_h, wh), (lin_h, wl), (lin_l, wh))):
                    last = t.matmul(at(name)[:], a[:, rows], w[:, part, cols], start=(part == 0 and i == 0),
                                    stop=(part == KC - 1 and i == 2))
                if part == KC - 1:
                    last.then_inc(bank_full[BANK[name]], 1)

            def x_T(b, _):
                pe.wait_ge(d_x[b.i], b.n2(16, 16))
                pe.wait_ge(*before("xT", b))
                blocks(at("xT"), lambda c: xb[b.i][:, c * P:(c + 1) * P]).then_inc(bank_full[BANK["xT"]], 1)

            def proj_q(b, part):
                if part == 0:
                    pe.wait_ge(*freed("xT", b))
                    pe.wait_ge(*before("q", b))
                linear("q", w_h, w_l, slice(0, D), part)

            def proj_k(b, part):
                if part == 0:
                    pe.wait_ge(*before("k", b))
                linear("k", w_h, w_l, slice(D, 2 * D), part)

            def proj_v(b, part):
                if part == 0:
                    pe.wait_ge(*before("v", b))
                linear("v", w_h, w_l, slice(2 * D, 3 * D), part)

            def parts_T(b, i):
                k, name = i // 2, f"tqk{i}"
                pe.wait_ge(s_part_l, b.n(2, k + 1))
                pe.wait_ge(*before(name, b))
                for h in range(8):
                    last = t.transpose(at(name)[0:SROWS, h * P // 2:(h + 1) * P // 2].bitcast(F16),
                                       qkn[k][:, 8 * (i % 2) + h, :, :].rearrange("p g d -> p (g d)"), ident16[:])
                last.then_inc(bank_full[BANK[name]], 1)

            def self_scores(b, c):
                name = f"s1m{c}"
                pe.wait_ge(*freed(f"tqk{c // 2}", b))
                pe.wait_ge(*freed(f"tqk{2 + c // 2}", b))
                pe.wait_ge(*before(name, b))
                t.matmul(at(name)[:].rearrange("p (h k) -> p h k", h=HC), identb[:],
                         maskb[:].unsqueeze(1).to_broadcast([P, HC, P]), start=True, stop=False)
                for j in range(HC):
                    last = t.matmul(at(name)[:, j * P:(j + 1) * P], qs[0:SROWS, HC * c + j, :],
                                    ks[0:SROWS, HC * c + j, :], start=False, stop=(j == HC - 1))
                last.then_inc(bank_full[BANK[name]], 1)

            def self_shift_T(b, _):
                pe.wait_ge(s_sh1, b.n(1, 1))
                pe.wait_ge(*before("m1T", b))
                t.transpose(at("m1T")[0:2 * NH, 0:P // 2].bitcast(F16), sh1[:].rearrange("p a h -> p (a h)"), ident16[:])\
                 .then_inc(bank_full[BANK["m1T"]], 1)

            def self_scores_T(b, c):
                name = f"s1t{c}"
                pe.wait_ge(d_sh1, b.n(16, 16))
                pe.wait_ge(*before(name, b))
                for j in range(HC):
                    last = t.matmul(at(name)[:, j * P:(j + 1) * P], ks[:, HC * c + j, :], qs[:, HC * c + j, :],
                                    start=True, stop=True)
                last.then_inc(bank_full[BANK[name]], 1)

            def self_pv(b, i):
                name = f"pv1{i}"
                pe.wait_ge(s_masked, b.n(KC, 2 * i + 2))
                pe.wait_ge(*freed("v", b))
                pe.wait_ge(*before(name, b))
                for h in range(8):
                    last = t.matmul(at(name)[:, h * (HD + 1):(h + 1) * (HD + 1)], p1[h // HC][:, h % HC, :],
                                    va[b.i][:, 8 * i + h, :], start=True, stop=True)
                last.then_inc(bank_full[BANK[name]], 1)

            def o_T(b, _):
                pe.wait_ge(*freed("pv10", b))
                pe.wait_ge(*freed("pv11", b))
                pe.wait_ge(*before("oT", b))
                blocks(at("oT"), lambda c: o1[:, c * P:(c + 1) * P]).then_inc(bank_full[BANK["oT"]], 1)

            def proj_o(b, part):
                if part == 0:
                    pe.wait_ge(*freed("oT", b))
                    pe.wait_ge(*before("wo", b))
                linear("wo", wo_h, wo_l, slice(0, D), part)

            def context_T(b, _):
                pe.wait_ge(d_cx, b.n(16, 16))
                pe.wait_ge(*before("vT", b))
                blocks(at("vT"), lambda c: cx[:, c * P:(c + 1) * P]).then_inc(bank_full[BANK["vT"]], 1)

            def cross_scores(b, n):
                h, c = n // KC, n % KC
                if n % (GH * KC) == 0:
                    pe.wait_ge(d_kst[b.i][h // GH], b.n2(80, 80))
                    pe.wait_ge(d_qst[b.i][h // GH], b.n2(80, 80))
                pe.wait_ge(mx_free, b.n(N_SC, n - 1))
                t.matmul(mx[n % 2][:], qst[b.i][0:XROWS, h, c * P:(c + 1) * P], kst[b.i][0:XROWS, h, :],
                         start=True, stop=True).then_inc(mx_full, 1)

            def cross_shift_T(b, g):
                pe.wait_ge(s_sh2, b.n(GROUPS, g + 1))
                pe.wait_ge(*before(f"mT{g}", b))
                t.transpose(at(f"mT{g}")[0:32, 0:P // 2].bitcast(F16), sh2[:, g].rearrange("p a h -> p (a h)"),
                            ident16[:]).then_inc(bank_full[BANK[f"mT{g}"]], 1)

            def cross_scores_T(b, n):
                unit, j = n // GH, n % GH
                g, i = unit // KC, unit % KC
                h = GH * g + j
                if n % (GH * KC) == 0:
                    pe.wait_ge(d_sh2[g], b.n(16, 16))
                pe.wait_ge(st_free, b.n(N_SC, n - 1))
                t.matmul(st[n % 2][:], kst[b.i][:, h, i * P:(i + 1) * P], qst[b.i][:, h, :],
                         start=True, stop=True).then_inc(st_full, 1)

            def cross_pv(b, unit):
                g, i = unit // KC, unit % KC
                pe.wait_ge(st_free, b.n(N_SC, GH * (unit + 1)))
                if unit == 0:
                    pe.wait_ge(*freed("vT", b))
                if i == 0:
                    pe.wait_ge(pv_free, b.n(GROUPS, g))
                for j in range(GH):
                    last = t.matmul(pv[32 * j:32 * j + 2 * XD, :], vT[b.i][:, i, GH * g + j, :],
                                    pp[:, unit % 2, j, :], start=(i == 0), stop=(i == KC - 1))
                last.then_inc(pv_unit, 1)

            def group_T(b, g):
                pe.wait_ge(pv_free, b.n(GROUPS, g + 1))
                pe.wait_ge(*before(f"o2T{g}", b))
                blocks(at(f"o2T{g}"), lambda c: o2[:, g, c * P:(c + 1) * P]).then_inc(bank_full[BANK[f"o2T{g}"]], 1)

            def back_T(b, _):
                for g in range(GROUPS):
                    pe.wait_ge(*freed(f"o2T{g}", b))
                pe.wait_ge(*before("o2N", b))
                blocks(at("o2N"), lambda c: o2n[:, c].rearrange("p h d -> p (h d)")).then_inc(bank_full[BANK["o2N"]], 1)

            def quant_T(b, _):
                pe.wait_ge(s_back, b.n(1, 1))
                pe.wait_ge(*before("xdT", b))
                blocks(at("xdT"), lambda c: yq[:, c * P:(c + 1) * P]).then_inc(bank_full[BANK["xdT"]], 1)

            def ffn(b, part):
                if part == 0:
                    pe.wait_ge(*freed("xdT", b))
                    pe.wait_ge(*before("ffn", b))
                linear("ffn", wf_h, wf_l, slice(0, D), part)

            run(pe, PE_STEPS, {
                "x_T": x_T, "proj_q": proj_q, "proj_k": proj_k, "proj_v": proj_v, "parts_T": parts_T,
                "self_scores": self_scores, "self_shift_T": self_shift_T, "self_scores_T": self_scores_T,
                "self_pv": self_pv, "o_T": o_T, "proj_o": proj_o, "context_T": context_T,
                "cross_scores": cross_scores, "cross_shift_T": cross_shift_T,
                "cross_scores_T": cross_scores_T, "cross_pv": cross_pv, "group_T": group_T,
                "back_T": back_T, "quant_T": quant_T, "ffn": ffn})


def kernel(x, ctx_2048, L0_attn_Wqkv, L0_attn_q_norm_w, L0_attn_k_norm_w, L0_attn_Wo, L0_ffn_weight):
    import numpy as np
    import concourse.bacc as bacc
    from concourse.bass_utils import run_bass_kernel_spmd

    S, HD = x.shape[1], x.shape[2] // 16
    inv_freq = (1.0 / 10000.0 ** (np.arange(0, HD, 2, dtype=np.float32) / np.float32(HD))).astype(np.float32)
    freqs = np.arange(S, dtype=np.float32)[:, None] * inv_freq[None, :]
    arrays = {
        "x": x, "ctx": ctx_2048, "wqkv": L0_attn_Wqkv, "q_norm_w": L0_attn_q_norm_w,
        "k_norm_w": L0_attn_k_norm_w, "wo": L0_attn_Wo, "wffn": L0_ffn_weight,
        "rope_cos": np.cos(freqs), "rope_sin": np.sin(freqs),
    }
    arrays = {k: np.ascontiguousarray(v) for k, v in arrays.items()}
    nc = bacc.Bacc("TRN2", target_bir_lowering=False, num_devices=1)
    args = [nc.dram_tensor(k, v.shape, mybir.dt.from_np(v.dtype), kind="ExternalInput").ap()
            for k, v in arrays.items()]
    out = nc.dram_tensor("out", x.shape, mybir.dt.float32, kind="ExternalOutput").ap()
    post_ln_decoder_kernel(nc, *args, out)
    r = run_bass_kernel_spmd(nc, [arrays], core_ids=[0])
    return r.results[0]["out"]
```

```python
import concourse.bass as bass
from concourse import mybir
from contextlib import ExitStack


def post_ln_decoder_kernel(nc, x, ctx_in, wqkv, q_norm_w, k_norm_w, wo, wffn, cos_t, sin_t, out):
    F32, F32R = mybir.dt.float32, mybir.dt.float32r
    BF16, F16, I32 = mybir.dt.bfloat16, mybir.dt.float16, mybir.dt.int32
    ALU, ACT, AX = mybir.AluOpType, mybir.ActivationFunctionType, mybir.AxisListType

    BATCH, TOK, D = x.shape
    P = TOK
    NH, HD = 16, D // 16
    HH = HD // 2
    XH, XD = 8, TOK // 8
    KC = D // P
    HC = NH // KC
    GROUPS, GH = XH // 4, 4
    UNITS = GROUPS * KC
    SELF_SCALE, CROSS_SCALE = HD ** -0.5, XD ** -0.5
    WINDOW = 256
    assert TOK <= WINDOW
    RMS_EPS, LN_EPS = 1e-6, 1e-5
    QBLK, FP8_MAX = 128, 448.0
    NQ = D // QBLK
    SHIFT_UNIT = 64.0
    NEG = -1e30
    SROWS = 3 * HD
    XROWS = 96
    Q_PLANE, K_PLANE = (0, 0, 0, 1, 1), (0, 1, 2, 0, 1)
    N_SC = XH * KC
    EXP_BITS = 0x7F800000
    MIN_NORMAL, MAGIC = 2.0 ** -6, 1.5 * 2.0 ** 20

    qpl_d = nc.dram_tensor("q_planes", [BATCH, 2, TOK, D], F16, kind="Internal").ap()
    kpl_d = nc.dram_tensor("k_planes", [BATCH, 3, TOK, D], BF16, kind="Internal").ap()
    x2_d = nc.dram_tensor("x2_rows", [BATCH, TOK, D], F32, kind="Internal").ap()
    sh1_d = nc.dram_tensor("self_shift", [BATCH, 2 * NH, TOK], F16, kind="Internal").ap()
    sh2_d = nc.dram_tensor("cross_shift", [BATCH, GROUPS, 32, P], F16, kind="Internal").ap()

    es = ExitStack()
    with es:
        def sb(name, shape, dt=F32):
            return es.enter_context(nc.sbuf_tensor(name, shape, dt))

        def bank(name):
            return es.enter_context(nc.psum_tensor(name, [P, 512], F32))

        def sem(name):
            return es.enter_context(nc.semaphore(name))

        w_h, w_l = sb("w_h", [P, KC, 3 * D], F32R), sb("w_l", [P, KC, 3 * D], F32R)
        wo_h, wo_l = sb("wo_h", [P, KC, D], F32R), sb("wo_l", [P, KC, D], F32R)
        wf_h, wf_l = sb("wf_h", [P, KC, D], F32R), sb("wf_l", [P, KC, D], F32R)
        cos_w = [sb(f"cos_w{i}", [P, NH, 2, HH]) for i in range(2)]
        sin_w = [sb(f"sin_w{i}", [P, NH, 2, HH]) for i in range(2)]
        cos_s, sin_s = sb("cos_s", [P, HH]), sb("sin_s", [P, HH])
        ident = sb("ident", [P, P])
        ident16 = sb("ident16", [P, P], F16)
        identb = sb("identb", [P, P], BF16)
        maskb = sb("maskb", [P, P], BF16)
        half = sb("half", [P, 1])
        xb = [sb(f"xb{i}", [P, D]) for i in range(2)]
        cx, cx_rest = sb("cx", [P, D]), sb("cx_rest", [P, D])
        lin_h, lin_l = sb("lin_h", [P, D], F32R), sb("lin_l", [P, D], F32R)
        ropeA, ropeB = sb("ropeA", [P, NH, 2, HH]), sb("ropeB", [P, NH, 2, HH])
        junk = sb("junk", [P, D], BF16)
        qkn = [sb(f"qkn{i}", [P, NH, 3, HD], F16) for i in range(2)]
        va = [sb(f"va{i}", [P, NH, HD]) for i in range(2)]
        ones = sb("ones", [P, HD])
        qs = sb("qs", [SROWS + 2, NH, P], F16)
        ks = sb("ks", [SROWS + 2, NH, P], F16)
        p1 = [sb(f"p1_{i}", [P, HC, P]) for i in range(2)]
        o1 = sb("o1", [P, D])
        x2 = sb("x2", [P, D])
        qpl = sb("qpl", [P, 2, D], F16)
        kpl = sb("kpl", [P, 3, D], BF16)
        qst = [sb(f"qst{i}", [XROWS + 2, XH, D], F16) for i in range(2)]
        kst = [sb(f"kst{i}", [XROWS + 2, XH, D], BF16) for i in range(2)]
        vT = [sb(f"vT{i}", [P, KC, XH, 2 * XD]) for i in range(2)]
        pp = sb("pp", [P, 2, GH, D])
        o2 = sb("o2", [P, GROUPS, D])
        x3 = sb("x3", [P, D])
        yq, yc = sb("yq", [P, D]), sb("yc", [P, D])
        o2n = yq[:].rearrange("p (c h d) -> p c h d", c=KC, h=XH)
        yout = sb("yout", [P, D])
        ssq, rms = sb("ssq", [P, 2]), sb("rms", [P, 2])
        nm1, sh1 = sb("nm1", [P, NH]), sb("sh1", [P, 2, NH], F16)
        sh1T = sb("sh1T", [2 * NH, P], F16)
        nm2, sh2 = sb("nm2", [P, GROUPS, 16]), sb("sh2", [P, GROUPS, 2, 16], F16)
        sh2T = [sb(f"sh2T{g}", [32, P], F16) for g in range(GROUPS)]
        st6 = [sb(f"st6_{i}", [P, 6]) for i in range(3)]
        mv = [sb(f"mv{i}", [P, 2]) for i in range(3)]
        rstd = [sb(f"rstd{i}", [P, 1]) for i in range(3)]
        r2 = sb("r2", [P, GROUPS, KC, GH])
        amax, qsc, qri = sb("amax", [P, NQ]), sb("qsc", [P, NQ]), sb("qri", [P, NQ])

        st = [bank(f"st{i}") for i in range(2)]
        pv = bank("pv")
        mx = [bank(f"mx{i}") for i in range(2)]
        banks = [bank(f"bank{i}") for i in range(3)]

        d_setup = [sem(f"d_setup{i}") for i in range(2)]
        d_const = sem("d_const")
        d_x = [sem(f"d_x{i}") for i in range(2)]
        d_cx, d_kpl_stored = sem("d_cx"), sem("d_kpl_stored")
        d_x2_stored, d_x3, d_qpl_stored = sem("d_x2_stored"), sem("d_x3"), sem("d_qpl_stored")
        d_qst = [[sem(f"d_qst{i}{g}") for g in range(GROUPS)] for i in range(2)]
        d_kst = [[sem(f"d_kst{i}{g}") for g in range(GROUPS)] for i in range(2)]
        d_sh1_stored, d_sh1 = sem("d_sh1_stored"), sem("d_sh1")
        d_sh2_stored = [sem(f"d_sh2_stored{g}") for g in range(GROUPS)]
        d_sh2 = [sem(f"d_sh2_{g}") for g in range(GROUPS)]
        d_out = sem("d_out")
        u_zero, u_const, u_dve = sem("u_zero"), sem("u_const"), sem("u_dve")
        u_staged, u_fT, u_done = sem("u_staged_used"), sem("u_ffn_transposed"), sem("u_done")
        bank_full = [sem(f"bank_full{i}") for i in range(3)]
        bank_free = [sem(f"bank_free{i}") for i in range(3)]
        mx_full, mx_free = sem("mx_full"), sem("mx_free")
        st_full, st_free = sem("st_full"), sem("st_free")
        pv_unit, pv_free = sem("pv_unit_done"), sem("pv_free")
        passed_sp, passed_pool, passed_dve = sem("passed_sp"), sem("passed_pool"), sem("passed_dve")
        s_xTh, s_oTh, s_xdh = sem("s_xT_high"), sem("s_oT_high"), sem("s_xdT_high")
        s_ssq, s_ms, s_rms = sem("s_ssq"), sem("s_mean_square"), sem("s_rms")
        s_rope, s_part_h, s_part_l = sem("s_rope"), sem("s_part_high"), sem("s_part_low")
        s_sc1, s_h1, s_sh1 = sem("s_shift1_scaled"), sem("s_shift1_high"), sem("s_shift1")
        s_sc2, s_h2, s_sh2 = sem("s_shift2_scaled"), sem("s_shift2_high"), sem("s_shift2")
        s_masked, s_r1, s_pv1, s_r2 = sem("s_masked"), sem("s_r1"), sem("s_self_pv"), sem("s_r2")
        s_oTl = sem("s_oT_low")
        s_st6, s_mv, s_ve, s_rstd, s_ln = ([sem(f"s_{n}{i}") for i in range(3)]
                                           for n in ("st6_", "mv", "ve", "rstd", "ln"))
        s_qh, s_ql = sem("s_q_high"), sem("s_q_low")
        s_k1, s_kr, s_k2, s_k3 = sem("s_k1"), sem("s_k_rest"), sem("s_k2"), sem("s_k3")
        s_am, s_qsc, s_qri = sem("s_amax"), sem("s_qscale"), sem("s_qrecip")
        s_unit, s_exp, s_magic, s_sum, s_round, s_back = (
            sem(f"s_quant_{n}") for n in ("unit", "exp", "magic", "sum", "round", "back"))

        def steps(text):
            out = []
            for word in text.split():
                name, rest = word.split(":")
                k, stage = rest.split("@")
                out.append((name, int(k), int(stage)))
            return out

        SP_STEPS = steps("""
            ld_cx:0@2 ld_qst:1@3 ld_kst:0@3 ld_x:0@0 st_sh2:1@4 ld_sh2:1@4 st_out:0@5 st_qpl:0@2
            st_sh1:0@1 ld_sh1:0@1 ld_qst:0@2 st_x2:0@2 ld_x2r:0@4 st_sh2:0@3 st_kpl:0@2 ld_sh2:0@3
            ld_kst:1@2""")
        POOL_STEPS = steps("""
            quant_unit:0@5 quant_round:0@5 quant_round:1@5 quant_round:2@5 layer_rstd:0@2
            context_rest:0@2 layer_rstd:2@5 query_low:0@2 mean_square:0@0 rope_sum:0@0 mean_square:1@0
            part_low:0@0 context_rest:1@2 mask:0@1 mask:1@1 rope_sum:1@0 mask:2@1 mask:3@1 part_low:1@0
            layer_rstd:1@4""")
        ACT_STEPS = steps("""
            probs:4@4 self_stack:2@1 probs:5@4 probs:6@4 probs:7@4 self_stack:3@1 probs:8@4 probs:9@4
            context_out:0@3 probs:10@4 probs:11@4 probs:12@4 probs:13@4 probs:14@4 xdT_high:0@5
            context_high:0@2 probs:15@4 xT_high:0@0 cross_shift_out:1@4 query_high:0@2 group_out:0@4
            square:0@0 self_shift_out:0@1 context_high:1@2 probs:16@4 square:1@0 part_high:0@0
            probs:17@4 probs:18@4 probs:19@4 value:0@0 self_probs:0@1 probs:20@4 self_probs:1@1
            probs:21@4 probs:22@4 self_probs:2@1 probs:23@4 self_probs:3@1 probs:24@4 probs:25@4
            self_stack:0@0 probs:26@4 probs:27@4 cross_shift_out:0@3 probs:28@4 probs:29@4 probs:30@4
            probs:31@4 part_high:1@0 oT_high:0@1 group_out:1@4 self_stack:1@0 probs:0@3 probs:1@3
            probs:2@3 probs:3@3""")
        DVE_STEPS = steps("""
            layernorm:1@5 quant_scale:0@5 add_self:0@2 quant_magic:0@5 cross_max:22@4 cross_max:23@4
            self_max:0@1 cross_max:24@4 cross_max:25@4 cross_max:26@4 cross_max:27@4 cross_max:28@4
            cross_max:29@4 xdT_low:0@5 self_max:1@1 cross_max:30@4 cross_max:31@4 self_max:2@1
            cross_shift:1@4 layernorm:0@2 cross_max:0@3 xT_low:0@0 add_ffn:0@5 self_max:3@1
            layernorm:2@5 cross_max:1@3 self_shift:0@1 cross_max:2@3 rope_terms:0@0 cross_max:3@3
            cross_max:4@3 cross_max:5@3 cross_max:6@3 cross_max:7@3 cross_max:8@3 rope_terms:1@0
            cross_max:9@3 cross_max:10@3 cross_max:11@3 cross_max:12@3 cross_max:13@3 cross_max:14@3
            cross_max:15@3 cross_shift:0@3 self_recip:0@1 self_recip:1@1 self_recip:2@1 self_recip:3@1
            cross_max:16@3 self_norm:0@1 cross_max:17@3 cross_norm:0@4 oT_low:0@1 cross_max:18@3
            cross_norm:1@4 cross_max:19@3 add_cross:0@4 cross_max:20@3 cross_max:21@3""")
        PE_STEPS = steps("""
            proj_o:3@2 context_T:0@3 cross_scores_T:5@4 cross_scores_T:6@4 cross_pv:0@4
            cross_scores_T:7@4 parts_T:3@1 cross_scores_T:8@4 cross_scores:23@4 self_scores:0@1
            cross_scores_T:9@4 cross_pv:1@4 cross_scores_T:10@4 cross_scores:24@4 cross_scores:25@4
            cross_scores_T:11@4 self_scores:1@1 cross_scores_T:12@4 cross_scores:26@4 self_scores:2@1
            cross_scores:27@4 cross_scores_T:13@4 cross_scores_T:14@4 cross_scores:28@4 quant_T:0@5
            cross_scores:29@4 cross_scores_T:15@4 cross_pv:2@4 cross_scores:30@4 cross_scores:31@4
            ffn:0@5 ffn:1@5 ffn:2@5 ffn:3@5 x_T:0@0 cross_shift_T:1@4 cross_scores:0@3 cross_pv:3@4
            self_scores:3@1 cross_scores:1@3 proj_q:0@0 proj_q:1@0 proj_q:2@0 proj_q:3@0
            cross_scores:2@3 proj_k:0@0 proj_k:1@0 self_shift_T:0@1 proj_k:2@0 cross_scores:3@3
            proj_k:3@0 cross_scores_T:16@4 cross_scores:4@3 proj_v:0@0 cross_scores_T:17@4
            cross_scores:5@3 cross_scores_T:18@4 cross_scores:6@3 proj_v:1@0 cross_scores:7@3
            proj_v:2@0 cross_scores:8@3 cross_scores_T:19@4 cross_scores:9@3 cross_scores_T:20@4
            proj_v:3@0 self_scores_T:0@1 cross_pv:4@4 cross_scores:10@3 self_scores_T:1@1
            cross_scores_T:21@4 cross_scores:11@3 cross_scores_T:22@4 self_scores_T:2@1
            cross_scores:12@3 self_pv:0@1 cross_scores:13@3 cross_scores_T:23@4 self_pv:1@1
            self_scores_T:3@1 cross_scores:14@3 cross_scores_T:24@4 cross_scores:15@3
            cross_scores_T:25@4 self_pv:2@1 parts_T:0@0 self_pv:3@1 cross_scores_T:26@4
            cross_scores_T:27@4 cross_pv:5@4 cross_shift_T:0@3 cross_scores_T:28@4 cross_scores_T:29@4
            group_T:0@4 cross_scores_T:30@4 cross_scores:16@3 cross_scores_T:31@4 cross_pv:6@4
            cross_scores:17@3 cross_pv:7@4 cross_scores:18@3 cross_scores:19@3 parts_T:1@0 group_T:1@4
            proj_o:0@1 cross_scores:20@3 cross_scores_T:0@3 cross_scores_T:1@3 back_T:0@4 parts_T:2@0
            proj_o:1@1 cross_scores_T:2@3 cross_scores:21@3 proj_o:2@1 cross_scores_T:3@3
            cross_scores:22@3 cross_scores_T:4@3""")

        BANK = {
            "xT": 1, "q": 1, "k": 0, "v": 2, "tqk0": 1, "tqk1": 2, "tqk2": 2, "tqk3": 2, "s1m0": 1,
            "s1m1": 0, "s1m2": 1, "s1m3": 0, "m1T": 2, "s1t0": 1, "s1t1": 0, "s1t2": 1, "s1t3": 1,
            "pvo": 0, "pvs": 2, "wo": 1, "vT": 0, "mT0": 1, "mT1": 0, "o2T0": 1, "o2T1": 0, "o2N": 0,
            "xdT": 2, "ffn": 2}
        OPENS = {("x_T", 0): "xT", ("proj_q", 0): "q", ("proj_k", 0): "k", ("proj_v", 0): "v",
                 ("self_shift_T", 0): "m1T", ("self_pv", 0): "pvo", ("proj_o", 0): "wo", ("context_T", 0): "vT",
                 ("back_T", 0): "o2N", ("quant_T", 0): "xdT", ("ffn", 0): "ffn"}
        OPENS.update({(name, k): f"{turn}{k}" for name, turn, n in (
            ("parts_T", "tqk", 4), ("self_scores", "s1m", KC), ("self_scores_T", "s1t", KC),
            ("cross_shift_T", "mT", GROUPS), ("group_T", "o2T", GROUPS))
            for k in range(n)})
        ALSO = {"pvo": ("pvs",)}
        TURNS = [[(turn, stage) for name, k, stage in PE_STEPS if (name, k) in OPENS
                  for turn in (OPENS[name, k],) + ALSO.get(OPENS[name, k], ()) if BANK[turn] == i]
                 for i in range(3)]

        LAST = max(stage for table in (SP_STEPS, POOL_STEPS, ACT_STEPS, DVE_STEPS, PE_STEPS)
                   for _, _, stage in table)
        SLOTS = BATCH + LAST
        LOOP0 = LAST + 3
        ROUNDS = (BATCH - LOOP0) // 2 - 1

        class Count:

            def __init__(self, b, rnd):
                self.b, self.rnd, self.i = b, rnd, b % 2

            def idx(self):
                return self.b if self.rnd is None else self.rnd * 2 + self.b

            def n(self, per, k):
                v = self.b * per + k
                return max(v, 0) if self.rnd is None else self.rnd * (2 * per) + v

            def n2(self, per, k):
                v = (self.b // 2) * per + k
                return v if self.rnd is None else self.rnd * per + v

        def turns_done(name, b, ahead=0, own=1):
            turns = TURNS[BANK[name]]
            at = [n for n, _ in turns].index(name)
            batch = b.b + ahead
            if batch < 0:
                return 0
            t = batch + turns[at][1]
            v = own + sum(0 <= t0 - stage < BATCH for t0 in range(t) for _, stage in turns)
            v += sum(0 <= t - stage < BATCH for _, stage in turns[:at])
            if b.rnd is None:
                return v
            assert t >= LAST and t + 2 * ROUNDS <= BATCH
            return b.rnd * (2 * len(turns)) + v

        class Point(tuple):

            def __new__(cls, sems, name, b, ahead, own):
                point = super().__new__(cls, (sems[BANK[name]], turns_done(name, b, ahead, own)))
                point.bank, point.order = BANK[name], turns_done(name, Count(b.b, None), ahead, own)
                return point

        def full(name, b, ahead=0):
            return Point(bank_full, name, b, ahead, 1)

        def freed(name, b, ahead=0):
            return Point(bank_free, name, b, ahead, 1)

        def before(name, b):
            return Point(bank_free, name, b, 0, 0)

        def last_of(*points):
            return [max((p for p in points if p.bank == i), key=lambda p: p.order)
                    for i in sorted({p.bank for p in points})]

        def run(eng, table, fns):
            def slot(t, rnd=None):
                for name, k, stage in table:
                    if 0 <= t - stage < BATCH:
                        fns[name](Count(t - stage, rnd), k)

            for t in range(LOOP0):
                slot(t)
            with eng.Fori(0, ROUNDS) as rnd:
                for u in range(2):
                    slot(LOOP0 + u, rnd)
            for t in range(LOOP0 + 2 * ROUNDS, SLOTS):
                slot(t)

        def at(name):
            return banks[BANK[name]]

        U_CONST = 4 + 1 + 4 * 2 + 2

        block = es.enter_context(nc.Block())

        @block.sync
        def _(sp):
            sp.dma_start(cos_s[:], cos_t).then_inc(d_const, 16)
            sp.dma_start(sin_s[:], sin_t).then_inc(d_const, 16)
            for dst, w in ((ropeA, q_norm_w), (ropeB, k_norm_w)):
                sp.dma_start(dst[:].rearrange("p h a d -> p (h a d)"), w.partition_broadcast(P)).then_inc(d_const, 16)
            for n in range(3 * KC):
                if n >= 2:
                    sp.wait_ge(u_staged, n - 1)
                src = (wqkv, wo, wffn)[n // KC][(n % KC) * P:(n % KC + 1) * P, :]
                sp.dma_start(pp[:, n % 2].rearrange("p a d -> p (a d)")[:, 0:src.shape[1]], src)\
                  .then_inc(d_setup[n % 2], 16)
            sp.wait_ge(u_const, U_CONST)

            def ld_x(b, _):
                sp.wait_ge(*freed("wo", b, -2))
                sp.sem_inc(passed_sp, 1)
                sp.dma_start(xb[b.i][:], x[b.idx()]).then_inc(d_x[b.i], 16)

            def ld_cx(b, _):
                sp.wait_ge(s_kr, b.n(1, 0))
                sp.sem_inc(passed_sp, 1)
                sp.wait_ge(*full("vT", b, -1))
                sp.sem_inc(passed_sp, 1)
                sp.dma_start(cx[:], ctx_in[b.idx()]).then_inc(d_cx, 16)

            def st_kpl(b, _):
                sp.wait_ge(s_k3, b.n(1, 1))
                sp.sem_inc(passed_sp, 1)
                sp.dma_start(kpl_d[b.idx()].rearrange("g p n -> p g n"), kpl[:]).then_inc(d_kpl_stored, 16)

            def ld_kst(b, g):
                sp.wait_ge(d_kpl_stored, b.n(16, 16))
                sp.sem_inc(passed_sp, 1)
                sp.wait_ge(st_full, b.n(N_SC, N_SC // GROUPS * (g + 1) - 2 * N_SC))
                sp.sem_inc(passed_sp, 1)
                for r in range(5):
                    sp.dma_start(kst[b.i][r * XD:(r + 1) * XD, GH * g:GH * (g + 1), :],
                                 kpl_d[b.idx()][K_PLANE[r]][GH * g * XD:GH * (g + 1) * XD, :]
                                 .rearrange("(h d) n -> d h n", d=XD)).then_inc(d_kst[b.i][g], 16)

            def ld_qst(b, g):
                sp.wait_ge(d_qpl_stored, b.n(16, 16))
                sp.sem_inc(passed_sp, 1)
                sp.wait_ge(st_full, b.n(N_SC, N_SC // GROUPS * (g + 1) - 2 * N_SC))
                sp.sem_inc(passed_sp, 1)
                for r in range(5):
                    sp.dma_start(qst[b.i][r * XD:(r + 1) * XD, GH * g:GH * (g + 1), :],
                                 qpl_d[b.idx()][Q_PLANE[r]][GH * g * XD:GH * (g + 1) * XD, :]
                                 .rearrange("(h d) n -> d h n", d=XD)).then_inc(d_qst[b.i][g], 16)

            def st_sh1(b, _):
                sp.wait_ge(*freed("m1T", b))
                sp.sem_inc(passed_sp, 1)
                sp.dma_start(sh1_d[b.idx()], sh1T[:]).then_inc(d_sh1_stored, 16)

            def ld_sh1(b, _):
                sp.wait_ge(d_sh1_stored, b.n(16, 16))
                sp.sem_inc(passed_sp, 1)
                sp.wait_ge(*full(f"s1t{KC - 1}", b, -1))
                sp.sem_inc(passed_sp, 1)
                sp.dma_start(qs[SROWS:SROWS + 2, :, :],
                             sh1_d[b.idx()].rearrange("(a h) q -> a h q", a=2)).then_inc(d_sh1, 16)

            def st_sh2(b, g):
                sp.wait_ge(*freed(f"mT{g}", b))
                sp.sem_inc(passed_sp, 1)
                sp.dma_start(sh2_d[b.idx()][g], sh2T[g][:]).then_inc(d_sh2_stored[g], 16)

            def ld_sh2(b, g):
                sp.wait_ge(d_sh2_stored[g], b.n(16, 16))
                sp.sem_inc(passed_sp, 1)
                sp.wait_ge(st_full, b.n(N_SC, N_SC // GROUPS * (g + 1) - 2 * N_SC))
                sp.sem_inc(passed_sp, 1)
                sp.dma_start(qst[b.i][XROWS:XROWS + 2, GH * g:GH * (g + 1), :]
                             .rearrange("a h (c m) -> a (h c) m", c=KC),
                             sh2_d[b.idx()][g].rearrange("(a r) m -> a r m", a=2)).then_inc(d_sh2[g], 16)

            def st_x2(b, _):
                sp.wait_ge(s_ln[0], b.n(1, 1))
                sp.sem_inc(passed_sp, 1)
                sp.dma_start(x2_d[b.idx()], x2[:]).then_inc(d_x2_stored, 16)

            def st_qpl(b, _):
                sp.wait_ge(s_ql, b.n(1, 1))
                sp.sem_inc(passed_sp, 1)
                sp.dma_start(qpl_d[b.idx()].rearrange("g p n -> p g n"), qpl[:]).then_inc(d_qpl_stored, 16)

            def ld_x2r(b, _):
                sp.wait_ge(d_x2_stored, b.n(16, 16))
                sp.sem_inc(passed_sp, 1)
                sp.wait_ge(*freed("ffn", b, -1))
                sp.sem_inc(passed_sp, 1)
                sp.dma_start(x3[:], x2_d[b.idx()]).then_inc(d_x3, 16)

            def st_out(b, _):
                sp.wait_ge(s_ln[2], b.n(1, 1))
                sp.sem_inc(passed_sp, 1)
                sp.dma_start(out[b.idx()], yout[:]).then_inc(d_out, 16)

            run(sp, SP_STEPS, {
                "ld_x": ld_x, "ld_cx": ld_cx, "st_kpl": st_kpl, "ld_kst": ld_kst, "ld_qst": ld_qst,
                "st_sh1": st_sh1, "ld_sh1": ld_sh1, "st_sh2": st_sh2, "ld_sh2": ld_sh2,
                "st_x2": st_x2, "st_qpl": st_qpl, "ld_x2r": ld_x2r, "st_out": st_out})
            sp.wait_ge(d_out, 16 * BATCH)

        @block.gpsimd
        def _(pool):
            g_ = nc.gpsimd
            for m in (ident, ident16, identb, maskb):
                g_.memset(m[:], 0.0).then_inc(u_zero, 1)
            pool.wait_ge(u_zero, 4)
            for m in (ident, ident16, identb):
                g_.affine_select(out=m[:], in_=m[:], compare_op=ALU.not_equal, fill=1.0, base=0,
                                 pattern=[[-1, P]], channel_multiplier=1).then_inc(u_const, 1)
            g_.affine_select(out=maskb[:], in_=maskb[:], compare_op=ALU.is_ge, fill=NEG, base=0,
                             pattern=[[-1, P]], channel_multiplier=1).then_inc(u_const, 1)
            g_.memset(half[:], -0.5).then_inc(u_const, 1)
            n = 5
            for rows, value in [r for i in range(2) for r in (
                    (vT[i][:, :, :, XD:2 * XD], 1.0),
                    (qst[i][64:XROWS, :, :], 0.0), (kst[i][64:XROWS, :, :], 0.0),
                    (kst[i][XROWS:XROWS + 2, :, :], SHIFT_UNIT))] + [
                    (ones[:], 1.0), (ks[SROWS:SROWS + 2, :, :], SHIFT_UNIT)]:
                pool.wait_ge(u_const, n)
                g_.memset(rows, value).then_inc(u_const, 1)
                n += 1
            pool.wait_ge(u_const, U_CONST)
            pool.wait_ge(u_done, 1)

            def mean_square(b, k):
                pool.wait_ge(s_ssq, b.n(2, k + 1))
                pool.sem_inc(passed_pool, 1)
                g_.tensor_scalar(rms[:, k:k + 1], ssq[:, k:k + 1], 1.0 / D, RMS_EPS, ALU.mult, ALU.add)\
                  .then_inc(s_ms, 1)
                pool.wait_ge(s_ms, b.n(2, k + 1))
                g_.tensor_tensor(rms[:, k:k + 1], rms[:, k:k + 1], half[:], ALU.pow).then_inc(s_rms, 1)

            def layer_rstd(b, i):
                pool.wait_ge(s_mv[i], b.n(1, 1))
                pool.sem_inc(passed_pool, 1)
                g_.tensor_scalar(rstd[i][:], mv[i][:, 1:2], 1.0, LN_EPS, ALU.mult, ALU.add).then_inc(s_ve[i], 1)
                pool.wait_ge(s_ve[i], b.n(1, 1))
                g_.tensor_tensor(rstd[i][:], rstd[i][:], half[:], ALU.pow).then_inc(s_rstd[i], 1)

            def rope_sum(b, k):
                pool.wait_ge(*freed("qk"[k], b))
                g_.tensor_tensor(ropeA[:], ropeA[:], ropeB[:], ALU.add).then_inc(s_rope, 1)

            def part_low(b, k):
                pool.wait_ge(s_part_h, b.n(2, k + 1))
                g_.tensor_tensor(qkn[k][:, :, 2 - k, :], ropeA[:].rearrange("p h a d -> p h (a d)"),
                                 qkn[k][:, :, 0, :], ALU.subtract).then_inc(s_part_l, 1)

            def mask(b, c):
                pool.wait_ge(*freed(f"s1t{c}", b))
                pool.sem_inc(passed_pool, 1)
                g_.affine_select(out=p1[c % 2][:], in_=p1[c % 2][:], compare_op=ALU.is_ge, fill=0.0, base=0,
                                 pattern=[[0, HC], [1, P]], channel_multiplier=-1).then_inc(s_masked, 1)

            def context_rest(b, k):
                if k == 0:
                    pool.wait_ge(s_k1, b.n(1, 1))
                    g_.tensor_tensor(cx_rest[:], cx[:], kpl[:, 0, :], ALU.subtract).then_inc(s_kr, 1)
                else:
                    pool.wait_ge(s_k2, b.n(1, 1))
                    g_.tensor_tensor(kpl[:, 2, :], cx_rest[:], kpl[:, 1, :], ALU.subtract).then_inc(s_k3, 1)

            yq_blocks = yq[:].rearrange("p (n k) -> p n k", n=NQ)

            def quant_unit(b, _):
                pool.wait_ge(s_qri, b.n(1, 1))
                g_.tensor_tensor(yq_blocks, x3[:].rearrange("p (n k) -> p n k", n=NQ),
                                 qri[:].unsqueeze(2).to_broadcast([P, NQ, QBLK]), ALU.mult).then_inc(s_unit, 1)

            def quant_round(b, step):
                if step == 0:
                    pool.wait_ge(s_magic, b.n(1, 1))
                    g_.tensor_tensor(yq[:], yq[:], yc[:], ALU.add).then_inc(s_sum, 1)
                elif step == 1:
                    pool.wait_ge(s_sum, b.n(1, 1))
                    g_.tensor_tensor(yq[:], yq[:], yc[:], ALU.subtract).then_inc(s_round, 1)
                else:
                    pool.wait_ge(s_round, b.n(1, 1))
                    g_.tensor_tensor(yq_blocks, yq_blocks, qsc[:].unsqueeze(2).to_broadcast([P, NQ, QBLK]), ALU.mult)\
                      .then_inc(s_back, 1)

            def query_low(b, _):
                pool.wait_ge(s_qh, b.n(1, 1))
                g_.tensor_tensor(qpl[:, 1, :], x2[:], qpl[:, 0, :], ALU.subtract).then_inc(s_ql, 1)

            run(pool, POOL_STEPS, {
                "mean_square": mean_square, "layer_rstd": layer_rstd, "rope_sum": rope_sum,
                "part_low": part_low, "mask": mask, "context_rest": context_rest,
                "quant_unit": quant_unit, "quant_round": quant_round, "query_low": query_low})

        @block.scalar
        def _(act):
            a = nc.scalar
            act.wait_ge(u_done, 1)
            act.wait_ge(u_const, U_CONST)

            def probs(b, n):
                unit, j = n // GH, n % GH
                act.wait_ge(st_full, b.n(N_SC, n + 1))
                act.wait_ge(pv_unit, b.n(UNITS, unit - 1))
                a.activation(pp[:, unit % 2, j, :], st[n % 2][:], ACT.Exp, scale=CROSS_SCALE).then_inc(st_free, 1)

            def group_out(b, g):
                act.wait_ge(pv_unit, b.n(UNITS, KC * (g + 1)))
                act.wait_ge(*full(f"o2T{g}", b, -1))
                a.activation(o2[:, g, :], pv[:], ACT.Copy).then_inc(pv_free, 1)

            def xT_high(b, _):
                act.wait_ge(*full("xT", b))
                a.activation(lin_h[:], at("xT")[:], ACT.Copy).then_inc(s_xTh, 1)

            def square(b, k):
                act.wait_ge(*full("qk"[k], b))
                act.wait_ge(s_ms, b.n(2, k - 1))
                act.wait_ge(s_ssq, b.n(2, k))
                a.activation(junk[:], at("qk"[k])[:], ACT.Square, accum_out=ssq[:, k:k + 1]).then_inc(s_ssq, 1)

            def part_high(b, k):
                act.wait_ge(s_rope, b.n(2, k + 1))
                act.wait_ge(*full(f"tqk{2 * k + 1}", b, -1))
                src = ropeA[:].rearrange("p h a d -> p h (a d)")
                a.activation(qkn[k][:, :, 0, :], src, ACT.Copy)
                a.activation(qkn[k][:, :, 1 + k, :], src, ACT.Copy).then_inc(s_part_h, 1)

            def value(b, _):
                for point in last_of(
                        full("v", b),
                        full("pvo", b, -2),
                ):
                    act.wait_ge(*point)
                a.activation(va[b.i][:], at("v")[:].rearrange("p (h d) -> p h d", h=NH), ACT.Copy)\
                 .then_inc(bank_free[BANK["v"]], 1)

            def self_stack(b, i):
                for point in last_of(
                        full(f"tqk{i}", b),
                        full(f"s1t{2 * (i % 2) + 1}", b, -1),
                ):
                    act.wait_ge(*point)
                dst = (qs, ks)[i // 2][0:SROWS, 8 * (i % 2):8 * (i % 2) + 8, :]
                a.activation(dst, at(f"tqk{i}")[0:SROWS, :].bitcast(F16).rearrange("p (h t) -> p h t", h=8), ACT.Copy)\
                 .then_inc(bank_free[BANK[f"tqk{i}"]], 1)

            def self_shift_out(b, _):
                act.wait_ge(*full("m1T", b))
                act.wait_ge(d_sh1_stored, b.n(16, 0))
                a.activation(sh1T[:], at("m1T")[0:2 * NH, 0:P // 2].bitcast(F16), ACT.Copy)\
                 .then_inc(bank_free[BANK["m1T"]], 1)

            def self_probs(b, c):
                if c == 1:
                    for point in last_of(full(f"s1t{c}", b), full("pvs", b, -1)):
                        act.wait_ge(*point)
                else:
                    act.wait_ge(*full(f"s1t{c}", b))
                    act.wait_ge(s_pv1, b.n(KC - 1, max(c - 1, 0)))
                a.activation(p1[c % 2][:], at(f"s1t{c}")[:].rearrange("p (h q) -> p h q", h=HC), ACT.Exp,
                             scale=SELF_SCALE).then_inc(bank_free[BANK[f"s1t{c}"]], 1)

            def oT_high(b, _):
                act.wait_ge(*freed("pvo", b))
                a.activation(lin_h[:], o1[:], ACT.Copy).then_inc(s_oTh, 1)

            def query_high(b, _):
                act.wait_ge(s_ln[0], b.n(1, 1))
                act.wait_ge(d_qpl_stored, b.n(16, 0))
                a.activation(qpl[:, 0, :], x2[:], ACT.Copy).then_inc(s_qh, 1)

            def context_high(b, k):
                if k == 0:
                    act.wait_ge(d_cx, b.n(16, 16))
                    act.wait_ge(d_kpl_stored, b.n(16, 0))
                    a.activation(kpl[:, 0, :], cx[:], ACT.Copy).then_inc(s_k1, 1)
                else:
                    act.wait_ge(s_kr, b.n(1, 1))
                    a.activation(kpl[:, 1, :], cx_rest[:], ACT.Copy).then_inc(s_k2, 1)

            def context_out(b, _):
                act.wait_ge(*full("vT", b))
                act.wait_ge(pv_unit, b.n(UNITS, -UNITS))
                a.activation(vT[b.i][:, :, :, 0:XD], at("vT")[:].rearrange("p (i h d) -> p i h d", i=KC, h=XH),
                             ACT.Copy).then_inc(bank_free[BANK["vT"]], 1)

            def cross_shift_out(b, g):
                act.wait_ge(*full(f"mT{g}", b))
                act.wait_ge(d_sh2_stored[g], b.n(16, 0))
                a.activation(sh2T[g][:], at(f"mT{g}")[0:32, 0:P // 2].bitcast(F16), ACT.Copy)\
                 .then_inc(bank_free[BANK[f"mT{g}"]], 1)

            def xdT_high(b, _):
                act.wait_ge(*full("xdT", b))
                a.activation(lin_h[:], at("xdT")[:], ACT.Copy).then_inc(s_xdh, 1)

            run(act, ACT_STEPS, {
                "probs": probs, "group_out": group_out, "xT_high": xT_high, "square": square,
                "part_high": part_high, "value": value, "self_stack": self_stack,
                "self_shift_out": self_shift_out, "self_probs": self_probs, "oT_high": oT_high,
                "query_high": query_high, "context_high": context_high, "context_out": context_out,
                "cross_shift_out": cross_shift_out, "xdT_high": xdT_high})

        @block.vector
        def _(dve):
            v = nc.vector
            done = [0]

            def step(ins):
                done[0] += 1
                ins.then_inc(u_dve, 1)
                dve.wait_ge(u_dve, done[0])

            dve.wait_ge(d_const, 64)
            for i, w in enumerate((ropeA, ropeB)):
                v.tensor_tensor(cos_w[i][:], w[:], cos_s[:].unsqueeze(1).unsqueeze(1).to_broadcast([P, NH, 2, HH]),
                                ALU.mult)
                sin_b = sin_s[:].unsqueeze(1).to_broadcast([P, NH, HH])
                v.scalar_tensor_tensor(sin_w[i][:, :, 0, :], w[:, :, 1, :], -1.0, sin_b, ALU.mult, ALU.mult)
                step(v.tensor_tensor(sin_w[i][:, :, 1, :], w[:, :, 0, :], sin_b, ALU.mult))
            for n in range(3 * KC):
                c, piece = n % KC, pp[:, n % 2].rearrange("p a d -> p (a d)")
                dve.wait_ge(d_setup[n % 2], 16 * (n // 2 + 1))
                if n < 2 * KC:
                    hi, lo = ((w_h, w_l), (wo_h, wo_l))[n // KC]
                    src = piece[:, 0:hi.shape[2]]
                    step(v.tensor_copy(hi[:, c, :], src))
                    v.tensor_tensor(lo[:, c, :], src, hi[:, c, :].bitcast(F32), ALU.subtract).then_inc(u_staged, 1)
                    continue
                src = piece[:, 0:D].rearrange("p (n k) -> p n k", n=NQ)
                y3 = yq[:].rearrange("p (n k) -> p n k", n=NQ)
                if c:
                    dve.wait_ge(u_fT, c)
                step(v.tensor_reduce(amax[:], src, AX.X, ALU.max, apply_absolute_value=True))
                step(v.tensor_scalar(qsc[:], amax[:], 1.0 / FP8_MAX, None, ALU.mult))
                step(v.reciprocal(qri[:], qsc[:]))
                step(v.tensor_tensor(y3, src, qri[:].unsqueeze(2).to_broadcast([P, NQ, QBLK]), ALU.mult))
                step(v.tensor_scalar(yc[:].bitcast(I32), yq[:].bitcast(I32), EXP_BITS, None, ALU.bitwise_and))
                step(v.tensor_scalar(yc[:], yc[:], MIN_NORMAL, MAGIC, ALU.max, ALU.mult))
                step(v.tensor_tensor(yq[:], yq[:], yc[:], ALU.add))
                step(v.tensor_tensor(yq[:], yq[:], yc[:], ALU.subtract))
                v.tensor_tensor(y3, y3, qsc[:].unsqueeze(2).to_broadcast([P, NQ, QBLK]), ALU.mult)\
                 .then_inc(u_staged, 1)
                dve.wait_ge(u_fT, c + 1)
                t4 = mx[0][:].rearrange("p (k o) -> p k o", k=KC)
                cols = slice(c * P, (c + 1) * P)
                step(v.tensor_copy(wf_h[:, :, cols], t4))
                step(v.tensor_tensor(wf_l[:, :, cols], t4, wf_h[:, :, cols].bitcast(F32), ALU.subtract))
            v.memset(amax[:], 0.0).then_inc(u_done, 1)
            dve.wait_ge(u_done, 1)

            def cross_max(b, n):
                dve.wait_ge(mx_full, b.n(N_SC, n + 1))
                v.tensor_reduce(nm2[:, n // 16, n % 16:n % 16 + 1], mx[n % 2][:], AX.X, ALU.max, negate=True)\
                 .then_inc(mx_free, 1)

            def cross_shift(b, g):
                dve.wait_ge(mx_free, b.n(N_SC, 16 * (g + 1)))
                v.tensor_scalar(nm2[:, g, :], nm2[:, g, :], 1.0 / SHIFT_UNIT, None, ALU.mult).then_inc(s_sc2, 1)
                dve.wait_ge(s_sc2, b.n(GROUPS, g + 1))
                v.tensor_copy(sh2[:, g, 0, :], nm2[:, g, :]).then_inc(s_h2, 1)
                dve.wait_ge(s_h2, b.n(GROUPS, g + 1))
                v.tensor_tensor(sh2[:, g, 1, :], nm2[:, g, :], sh2[:, g, 0, :], ALU.subtract).then_inc(s_sh2, 1)

            def self_max(b, c):
                dve.wait_ge(*full(f"s1m{c}", b))
                v.tensor_reduce(nm1[:, HC * c:HC * (c + 1)], at(f"s1m{c}")[:].rearrange("p (h k) -> p h k", h=HC),
                                AX.X, ALU.max, negate=True).then_inc(bank_free[BANK[f"s1m{c}"]], 1)

            def self_shift(b, _):
                for point in last_of(*(freed(f"s1m{c}", b) for c in range(KC))):
                    dve.wait_ge(*point)
                v.tensor_scalar(nm1[:], nm1[:], 1.0 / SHIFT_UNIT, None, ALU.mult).then_inc(s_sc1, 1)
                dve.wait_ge(s_sc1, b.n(1, 1))
                v.tensor_copy(sh1[:, 0, :], nm1[:]).then_inc(s_h1, 1)
                dve.wait_ge(s_h1, b.n(1, 1))
                v.tensor_tensor(sh1[:, 1, :], nm1[:], sh1[:, 0, :], ALU.subtract).then_inc(s_sh1, 1)

            def xT_low(b, _):
                dve.wait_ge(s_xTh, b.n(1, 1))
                v.tensor_tensor(lin_l[:], at("xT")[:], lin_h[:].bitcast(F32), ALU.subtract)\
                 .then_inc(bank_free[BANK["xT"]], 1)

            def rope_terms(b, k):
                dve.wait_ge(s_rms, b.n(2, k + 1))
                dve.wait_ge(s_part_l, b.n(2, k))
                rows = at("qk"[k])
                src = rows[:].rearrange("p (h a d) -> p h a d", h=NH, a=2)
                v.scalar_tensor_tensor(ropeA[:].rearrange("p h a d -> p (h a d)"), rows[:], rms[:, k:k + 1],
                                       cos_w[k][:].rearrange("p h a d -> p (h a d)"), ALU.mult, ALU.mult)
                v.scalar_tensor_tensor(ropeB[:, :, 0, :], src[:, :, 1, :], rms[:, k:k + 1], sin_w[k][:, :, 0, :],
                                       ALU.mult, ALU.mult)
                v.scalar_tensor_tensor(ropeB[:, :, 1, :], src[:, :, 0, :], rms[:, k:k + 1], sin_w[k][:, :, 1, :],
                                       ALU.mult, ALU.mult).then_inc(bank_free[BANK["qk"[k]]], 1)

            def self_recip(b, c):
                dve.wait_ge(*full("pvs", b))
                cols = slice(c * P, (c + 1) * P)
                done = s_r1 if c < KC - 1 else bank_free[BANK["pvs"]]
                v.reciprocal(o1[:, cols], at("pvs")[:, cols]).then_inc(done, 1)

            def self_norm(b, _):
                dve.wait_ge(*full("pvo", b))
                dve.wait_ge(s_r1, b.n(KC - 1, KC - 1))
                dve.wait_ge(*freed("pvs", b))
                v.tensor_tensor(o1[:], at("pvo")[:], o1[:], ALU.mult).then_inc(bank_free[BANK["pvo"]], 1)

            def oT_low(b, _):
                dve.wait_ge(s_oTh, b.n(1, 1))
                v.tensor_tensor(lin_l[:], o1[:], lin_h[:].bitcast(F32), ALU.subtract).then_inc(s_oTl, 1)

            def layernorm_stats(b, i, rows):
                v.bn_stats(st6[i][:], rows[:]).then_inc(s_st6[i], 1)
                dve.wait_ge(s_st6[i], b.n(1, 1))
                dve.sem_inc(passed_dve, 1)
                v.bn_aggr(mv[i][:], st6[i][:]).then_inc(s_mv[i], 1)

            def layernorm(b, i):
                rows = (x2, x3, yout)[i]
                dve.wait_ge(s_rstd[i], b.n(1, 1))
                v.tensor_scalar(rows[:], rows[:], mv[i][:, 0:1], rstd[i][:], ALU.subtract, ALU.mult)\
                 .then_inc(s_ln[i], 1)

            def add_self(b, _):
                dve.wait_ge(*full("wo", b))
                dve.wait_ge(d_x2_stored, b.n(16, 0))
                dve.wait_ge(s_ql, b.n(1, 0))
                v.tensor_tensor(x2[:], at("wo")[:], xb[b.i][:], ALU.add).then_inc(bank_free[BANK["wo"]], 1)
                dve.wait_ge(*freed("wo", b))
                layernorm_stats(b, 0, x2)

            def cross_norm(b, g):
                dve.wait_ge(*full(f"o2T{g}", b))
                src = at(f"o2T{g}")[:].rearrange("p (c j d) -> p c j d", c=KC, j=GH)
                v.reciprocal(r2[:, g].unsqueeze(3), src[:, :, :, XD:XD + 1]).then_inc(s_r2, 1)
                dve.wait_ge(s_r2, b.n(GROUPS, g + 1))
                dve.wait_ge(*full("xdT", b, -1))
                v.tensor_tensor(o2n[:, :, GH * g:GH * (g + 1), :], src[:, :, :, 0:XD],
                                r2[:, g].unsqueeze(3).to_broadcast([P, KC, GH, XD]), ALU.mult)\
                 .then_inc(bank_free[BANK[f"o2T{g}"]], 1)

            def add_cross(b, _):
                dve.wait_ge(*full("o2N", b))
                dve.wait_ge(d_x3, b.n(16, 16))
                v.tensor_tensor(x3[:], at("o2N")[:], x3[:], ALU.add).then_inc(bank_free[BANK["o2N"]], 1)
                dve.wait_ge(*freed("o2N", b))
                layernorm_stats(b, 1, x3)

            def quant_scale(b, _):
                dve.wait_ge(s_ln[1], b.n(1, 1))
                v.tensor_reduce(amax[:], x3[:].rearrange("p (n k) -> p n k", n=NQ), AX.X, ALU.max,
                                apply_absolute_value=True).then_inc(s_am, 1)
                dve.wait_ge(s_am, b.n(1, 1))
                v.tensor_scalar(qsc[:], amax[:], 1.0 / FP8_MAX, None, ALU.mult).then_inc(s_qsc, 1)
                dve.wait_ge(s_qsc, b.n(1, 1))
                v.reciprocal(qri[:], qsc[:]).then_inc(s_qri, 1)

            def quant_magic(b, _):
                dve.wait_ge(s_unit, b.n(1, 1))
                v.tensor_scalar(yc[:].bitcast(I32), yq[:].bitcast(I32), EXP_BITS, None, ALU.bitwise_and)\
                 .then_inc(s_exp, 1)
                dve.wait_ge(s_exp, b.n(1, 1))
                v.tensor_scalar(yc[:], yc[:], MIN_NORMAL, MAGIC, ALU.max, ALU.mult).then_inc(s_magic, 1)

            def xdT_low(b, _):
                dve.wait_ge(s_xdh, b.n(1, 1))
                v.tensor_tensor(lin_l[:], at("xdT")[:], lin_h[:].bitcast(F32), ALU.subtract)\
                 .then_inc(bank_free[BANK["xdT"]], 1)

            def add_ffn(b, _):
                dve.wait_ge(*full("ffn", b))
                dve.wait_ge(d_out, b.n(16, 0))
                v.tensor_tensor(yout[:], at("ffn")[:], x3[:], ALU.add).then_inc(bank_free[BANK["ffn"]], 1)
                dve.wait_ge(*freed("ffn", b))
                layernorm_stats(b, 2, yout)

            run(dve, DVE_STEPS, {
                "cross_max": cross_max, "cross_shift": cross_shift, "self_max": self_max,
                "self_shift": self_shift, "xT_low": xT_low, "rope_terms": rope_terms,
                "self_recip": self_recip, "self_norm": self_norm, "oT_low": oT_low,
                "layernorm": layernorm, "add_self": add_self,
                "cross_norm": cross_norm, "add_cross": add_cross, "quant_scale": quant_scale,
                "quant_magic": quant_magic, "xdT_low": xdT_low, "add_ffn": add_ffn})

        @block.tensor
        def _(pe):
            t = nc.tensor
            pe.wait_ge(u_const, U_CONST)
            for c in range(KC):
                pe.wait_ge(u_staged, 2 * KC + c + 1)
                for k in range(KC):
                    last = t.transpose(mx[0][:, k * P:(k + 1) * P], yq[:, k * P:(k + 1) * P], ident[:])
                last.then_inc(u_fT, 1)
            pe.wait_ge(u_done, 1)

            def blocks(dst, src, idm=ident):
                for c in range(KC):
                    last = t.transpose(dst[:, c * P:(c + 1) * P], src(c), idm[:])
                return last

            def linear(name, wh, wl, cols, part):
                rows = slice(part * P, (part + 1) * P)
                for i, (a, w) in enumerate(((lin_h, wh), (lin_h, wl), (lin_l, wh))):
                    last = t.matmul(at(name)[:], a[:, rows], w[:, part, cols], start=(part == 0 and i == 0),
                                    stop=(part == KC - 1 and i == 2))
                if part == KC - 1:
                    last.then_inc(bank_full[BANK[name]], 1)

            def x_T(b, _):
                pe.wait_ge(d_x[b.i], b.n2(16, 16))
                pe.wait_ge(*before("xT", b))
                blocks(at("xT"), lambda c: xb[b.i][:, c * P:(c + 1) * P]).then_inc(bank_full[BANK["xT"]], 1)

            def proj_q(b, part):
                if part == 0:
                    for point in last_of(
                            freed("xT", b),
                            before("q", b),
                    ):
                        pe.wait_ge(*point)
                linear("q", w_h, w_l, slice(0, D), part)

            def proj_k(b, part):
                if part == 0:
                    pe.wait_ge(*before("k", b))
                linear("k", w_h, w_l, slice(D, 2 * D), part)

            def proj_v(b, part):
                if part == 0:
                    pe.wait_ge(*before("v", b))
                linear("v", w_h, w_l, slice(2 * D, 3 * D), part)

            def parts_T(b, i):
                k, name = i // 2, f"tqk{i}"
                pe.wait_ge(s_part_l, b.n(2, k + 1))
                pe.wait_ge(*before(name, b))
                for h in range(8):
                    last = t.transpose(at(name)[0:SROWS, h * P // 2:(h + 1) * P // 2].bitcast(F16),
                                       qkn[k][:, 8 * (i % 2) + h, :, :].rearrange("p g d -> p (g d)"), ident16[:])
                last.then_inc(bank_full[BANK[name]], 1)

            def self_scores(b, c):
                name = f"s1m{c}"
                for point in last_of(
                        freed(f"tqk{c // 2}", b),
                        freed(f"tqk{2 + c // 2}", b),
                        before(name, b),
                ):
                    pe.wait_ge(*point)
                t.matmul(at(name)[:].rearrange("p (h k) -> p h k", h=HC), identb[:],
                         maskb[:].unsqueeze(1).to_broadcast([P, HC, P]), start=True, stop=False)
                for j in range(HC):
                    last = t.matmul(at(name)[:, j * P:(j + 1) * P], qs[0:SROWS, HC * c + j, :],
                                    ks[0:SROWS, HC * c + j, :], start=False, stop=(j == HC - 1))
                last.then_inc(bank_full[BANK[name]], 1)

            def self_shift_T(b, _):
                pe.wait_ge(s_sh1, b.n(1, 1))
                pe.wait_ge(*before("m1T", b))
                t.transpose(at("m1T")[0:2 * NH, 0:P // 2].bitcast(F16), sh1[:].rearrange("p a h -> p (a h)"), ident16[:])\
                 .then_inc(bank_full[BANK["m1T"]], 1)

            def self_scores_T(b, c):
                name = f"s1t{c}"
                pe.wait_ge(d_sh1, b.n(16, 16))
                pe.wait_ge(*before(name, b))
                for j in range(HC):
                    last = t.matmul(at(name)[:, j * P:(j + 1) * P], ks[:, HC * c + j, :], qs[:, HC * c + j, :],
                                    start=True, stop=True)
                last.then_inc(bank_full[BANK[name]], 1)

            def self_pv(b, c):
                pe.wait_ge(s_masked, b.n(KC, c + 1))
                if c == 0:
                    for point in last_of(
                            freed("v", b),
                            before("pvo", b),
                            before("pvs", b),
                    ):
                        pe.wait_ge(*point)
                cols = slice(c * P, (c + 1) * P)
                for j in range(HC):
                    last_v = t.matmul(at("pvo")[HD * j:HD * (j + 1), cols], va[b.i][:, HC * c + j, :],
                                      p1[c % 2][:, j, :], start=True, stop=True)
                for j in range(HC):
                    last = t.matmul(at("pvs")[HD * j:HD * (j + 1), cols], ones[:], p1[c % 2][:, j, :],
                                    start=True, stop=True)
                if c == KC - 1:
                    last_v.then_inc(bank_full[BANK["pvo"]], 1)
                    last.then_inc(bank_full[BANK["pvs"]], 1)
                else:
                    last.then_inc(s_pv1, 1)

            def proj_o(b, part):
                if part == 0:
                    pe.wait_ge(s_oTl, b.n(1, 1))
                    pe.wait_ge(*before("wo", b))
                linear("wo", wo_h, wo_l, slice(0, D), part)

            def context_T(b, _):
                pe.wait_ge(d_cx, b.n(16, 16))
                pe.wait_ge(*before("vT", b))
                blocks(at("vT"), lambda c: cx[:, c * P:(c + 1) * P]).then_inc(bank_full[BANK["vT"]], 1)

            def cross_scores(b, n):
                h, c = n // KC, n % KC
                if n % (GH * KC) == 0:
                    pe.wait_ge(d_kst[b.i][h // GH], b.n2(80, 80))
                    pe.wait_ge(d_qst[b.i][h // GH], b.n2(80, 80))
                pe.wait_ge(mx_free, b.n(N_SC, n - 1))
                t.matmul(mx[n % 2][:], qst[b.i][0:XROWS, h, c * P:(c + 1) * P], kst[b.i][0:XROWS, h, :],
                         start=True, stop=True).then_inc(mx_full, 1)

            def cross_shift_T(b, g):
                pe.wait_ge(s_sh2, b.n(GROUPS, g + 1))
                pe.wait_ge(*before(f"mT{g}", b))
                t.transpose(at(f"mT{g}")[0:32, 0:P // 2].bitcast(F16), sh2[:, g].rearrange("p a h -> p (a h)"),
                            ident16[:]).then_inc(bank_full[BANK[f"mT{g}"]], 1)

            def cross_scores_T(b, n):
                unit, j = n // GH, n % GH
                g, i = unit // KC, unit % KC
                h = GH * g + j
                if n % (GH * KC) == 0:
                    pe.wait_ge(d_sh2[g], b.n(16, 16))
                pe.wait_ge(st_free, b.n(N_SC, n - 1))
                t.matmul(st[n % 2][:], kst[b.i][:, h, i * P:(i + 1) * P], qst[b.i][:, h, :],
                         start=True, stop=True).then_inc(st_full, 1)

            def cross_pv(b, unit):
                g, i = unit // KC, unit % KC
                pe.wait_ge(st_free, b.n(N_SC, GH * (unit + 1)))
                if unit == 0:
                    pe.wait_ge(*freed("vT", b))
                if i == 0:
                    pe.wait_ge(pv_free, b.n(GROUPS, g))
                for j in range(GH):
                    last = t.matmul(pv[32 * j:32 * j + 2 * XD, :], vT[b.i][:, i, GH * g + j, :],
                                    pp[:, unit % 2, j, :], start=(i == 0), stop=(i == KC - 1))
                last.then_inc(pv_unit, 1)

            def group_T(b, g):
                pe.wait_ge(pv_free, b.n(GROUPS, g + 1))
                pe.wait_ge(*before(f"o2T{g}", b))
                blocks(at(f"o2T{g}"), lambda c: o2[:, g, c * P:(c + 1) * P]).then_inc(bank_full[BANK[f"o2T{g}"]], 1)

            def back_T(b, _):
                for point in last_of(
                        *(freed(f"o2T{g}", b) for g in range(GROUPS)),
                        before("o2N", b),
                ):
                    pe.wait_ge(*point)
                blocks(at("o2N"), lambda c: o2n[:, c].rearrange("p h d -> p (h d)")).then_inc(bank_full[BANK["o2N"]], 1)

            def quant_T(b, _):
                pe.wait_ge(s_back, b.n(1, 1))
                pe.wait_ge(*before("xdT", b))
                blocks(at("xdT"), lambda c: yq[:, c * P:(c + 1) * P]).then_inc(bank_full[BANK["xdT"]], 1)

            def ffn(b, part):
                if part == 0:
                    for point in last_of(
                            freed("xdT", b),
                            before("ffn", b),
                    ):
                        pe.wait_ge(*point)
                linear("ffn", wf_h, wf_l, slice(0, D), part)

            run(pe, PE_STEPS, {
                "x_T": x_T, "proj_q": proj_q, "proj_k": proj_k, "proj_v": proj_v, "parts_T": parts_T,
                "self_scores": self_scores, "self_shift_T": self_shift_T, "self_scores_T": self_scores_T,
                "self_pv": self_pv, "proj_o": proj_o, "context_T": context_T,
                "cross_scores": cross_scores, "cross_shift_T": cross_shift_T,
                "cross_scores_T": cross_scores_T, "cross_pv": cross_pv, "group_T": group_T,
                "back_T": back_T, "quant_T": quant_T, "ffn": ffn})


def kernel(x, ctx_2048, L0_attn_Wqkv, L0_attn_q_norm_w, L0_attn_k_norm_w, L0_attn_Wo, L0_ffn_weight):
    import numpy as np
    import concourse.bacc as bacc
    from concourse.bass_utils import run_bass_kernel_spmd

    S, HD = x.shape[1], x.shape[2] // 16
    inv_freq = (1.0 / 10000.0 ** (np.arange(0, HD, 2, dtype=np.float32) / np.float32(HD))).astype(np.float32)
    freqs = np.arange(S, dtype=np.float32)[:, None] * inv_freq[None, :]
    arrays = {
        "x": x, "ctx": ctx_2048, "wqkv": L0_attn_Wqkv, "q_norm_w": L0_attn_q_norm_w,
        "k_norm_w": L0_attn_k_norm_w, "wo": L0_attn_Wo, "wffn": L0_ffn_weight,
        "rope_cos": np.cos(freqs), "rope_sin": np.sin(freqs),
    }
    arrays = {k: np.ascontiguousarray(v) for k, v in arrays.items()}
    nc = bacc.Bacc("TRN2", target_bir_lowering=False, num_devices=1)
    args = [nc.dram_tensor(k, v.shape, mybir.dt.from_np(v.dtype), kind="ExternalInput").ap()
            for k, v in arrays.items()]
    out = nc.dram_tensor("out", x.shape, mybir.dt.float32, kind="ExternalOutput").ap()
    post_ln_decoder_kernel(nc, *args, out)
    r = run_bass_kernel_spmd(nc, [arrays], core_ids=[0])
    return r.results[0]["out"]
```
